# Optimizing a Trainium2 kernel written in Bass

```python
import numpy as np
import jax
import jax.numpy as jnp

def _softmax(x, axis=-1):
    return jax.nn.softmax(x, axis=axis)
def _gelu(x):
    return jax.nn.gelu(x, approximate=True)
def _silu(x):
    return jax.nn.silu(x)
def _sigmoid(x):
    return jax.nn.sigmoid(x)
def _layernorm(x, axis=-1, eps=1e-5):
    m = jnp.mean(x, axis=axis, keepdims=True)
    v = jnp.var(x, axis=axis, keepdims=True)
    return (x - m) / jnp.sqrt(v + eps)
def _scatter_add(tgt, idx, src, axis=0):
    return tgt.at[idx].add(src)
def _segment_sum(src, seg, n):
    return jax.ops.segment_sum(src, seg, n)

kernel_name = 'mk_vit_tower_d1_tok_img512_1f1b4e'

def setup_inputs(seed: int = 0):
    np.random.seed(seed)
    _w = jnp.asarray
    def _rec_inputs():
        import jax
        import jax.numpy as jnp
        _rk = jax.random.key(seed)
        x = (0.000249115 + 0.999088 * jax.random.normal(jax.random.fold_in(_rk, 1), (32, 256, 257, 2), jnp.float32))
        return x
    x = _rec_inputs()
    def _L0_tok_setup():
        import jax, jax.numpy as jnp
        import numpy as np
        NLAT = 256
        NLON = 2 * NLAT
        LMAX = NLAT
        MMAX = NLAT + 1
        ALPHA = 2.0
        TAU = 3.0
        SIGMA = TAU ** (0.5 * (2 * ALPHA - 2.0))
        RADIUS = 1.0

        def _legpoly(mmax, lmax, x):
            nmax = max(mmax, lmax)
            vdm = np.zeros((nmax, nmax, len(x)), dtype=np.float64)
            norm_factor = 1.0 / np.sqrt(4.0 * np.pi)
            vdm[0, 0, :] = norm_factor / np.sqrt(4.0 * np.pi)
            for l in range(1, nmax):
                vdm[l - 1, l] = np.sqrt(2 * l + 1) * x * vdm[l - 1, l - 1]
                vdm[l, l] = np.sqrt((2 * l + 1) * (1 + x) * (1 - x) / (2 * l)) * vdm[l - 1, l - 1]
            for l in range(2, nmax):
                for m in range(0, l - 1):
                    a = np.sqrt((2 * l - 1) / (l - m) * (2 * l + 1) / (l + m))
                    b = np.sqrt((l + m - 1) / (l - m) * (2 * l + 1) / (2 * l - 3) * (l - m - 1) / (l + m))
                    vdm[m, l] = x * a * vdm[m, l - 1] - b * vdm[m, l - 2]
            vdm = vdm[:mmax, :lmax]
            for m in range(1, mmax, 2):
                vdm[m] *= -1.0
            return vdm

        def _make_buffers():
            tj = np.pi * np.arange(NLAT) / (NLAT - 1)
            x = np.flip(np.cos(tj)).copy()
            pct = _legpoly(MMAX, LMAX, x).astype(np.float32)
            l = np.arange(NLAT, dtype=np.float64)
            e = SIGMA * (l * (l + 1) / RADIUS ** 2 + TAU ** 2) ** (-ALPHA / 2.0)
            se = np.tril(np.repeat(e[:, None], NLAT + 1, axis=1))
            se[0, 0] = 0.0
            sqrt_eig = se[None].astype(np.float32)
            return (jnp.asarray(pct), jnp.asarray(sqrt_eig))
        key = jax.random.key(seed)
        xi = jax.random.normal(key, (8, NLAT, NLAT + 1, 2), dtype=jnp.float32)
        pct, sqrt_eig = _make_buffers()
        return {'xi': xi, 'sqrt_eig': sqrt_eig, 'pct': pct, 'N': 8}
    _L0_tok_all = _L0_tok_setup()
    _L0_tok_in = {k: v for k, v in _L0_tok_all.items() if k in ('sqrt_eig', 'pct', )}
    del _L0_tok_all

    def _L0_attn_setup():
        import jax, jax.numpy as jnp
        import numpy as np
        EPS = 1e-05
        H = 1

        def _silu(x):
            return x * jax.nn.sigmoid(x)

        def _causal_dwconv(x, w):
            K = w.shape[1]
            xp = jnp.pad(x, ((0, 0), (K - 1, 0), (0, 0)))
            out = jax.lax.conv_general_dilated(xp.transpose(0, 2, 1), w[:, None, :], (1,), 'VALID', dimension_numbers=('NCH', 'OIH', 'NCH'), feature_group_count=w.shape[0])
            return out.transpose(0, 2, 1)

        def _l2norm(x):
            return x * jax.lax.rsqrt(jnp.sum(x * x, -1, keepdims=True) + 1e-06)

        def _gated_delta_net(x, q_proj_w, k_proj_w, v_proj_w, b_proj_w, a_proj_w, A_log, dt_bias, q_conv_w, k_conv_w, v_conv_w, g_proj_w, o_norm_w, o_proj_w):
            B, T, D = x.shape
            Dh = D // H
            scale = Dh ** (-0.5)
            q = _silu(_causal_dwconv(x @ q_proj_w.T, q_conv_w))
            k = _silu(_causal_dwconv(x @ k_proj_w.T, k_conv_w))
            v = _silu(_causal_dwconv(x @ v_proj_w.T, v_conv_w))
            beta = jax.nn.sigmoid(x @ b_proj_w.T)
            g = -jnp.exp(A_log) * jax.nn.softplus(x @ a_proj_w.T + dt_bias)
            qh = _l2norm(q.reshape(B, T, H, Dh)) * scale
            kh = _l2norm(k.reshape(B, T, H, Dh))
            vh = v.reshape(B, T, H, Dh)
            xs = (jnp.moveaxis(qh, 1, 0), jnp.moveaxis(kh, 1, 0), jnp.moveaxis(vh, 1, 0), jnp.moveaxis(g, 1, 0), jnp.moveaxis(beta, 1, 0))

            def step(S, inp):
                q_t, k_t, v_t, g_t, b_t = inp
                S = S * jnp.exp(g_t)[..., None, None]
                kv = jnp.einsum('bhk,bhkv->bhv', k_t, S)
                dv = (v_t - kv) * b_t[..., None]
                S = S + k_t[..., None] * dv[..., None, :]
                o_t = jnp.einsum('bhk,bhkv->bhv', q_t, S)
                return (S, o_t)
            S0 = jnp.zeros((B, H, Dh, Dh), x.dtype)
            _, o = jax.lax.scan(step, S0, xs)
            o = jnp.moveaxis(o, 0, 1)
            gate = (x @ g_proj_w.T).reshape(B, T, H, Dh)
            o = o * jax.lax.rsqrt(jnp.mean(o * o, -1, keepdims=True) + EPS) * o_norm_w
            o = o * _silu(gate)
            return o.reshape(B, T, D) @ o_proj_w.T
        key = jax.random.key(seed)
        B, T, D, K = (2, 1024, 512, 4)
        ks = jax.random.split(key, 12)
        p = lambda k, shape, s=0.02: jax.random.normal(k, shape, jnp.float32) * s
        return {'x': jax.random.normal(ks[0], (B, T, D), jnp.float32), 'q_proj_w': p(ks[1], (D, D)), 'k_proj_w': p(ks[2], (D, D)), 'v_proj_w': p(ks[3], (D, D)), 'b_proj_w': p(ks[4], (H, D)), 'a_proj_w': p(ks[5], (H, D)), 'A_log': jnp.log(jax.random.uniform(ks[6], (H,), jnp.float32, 1.0, 16.0)), 'dt_bias': jnp.full((H,), -4.6, jnp.float32), 'q_conv_w': p(ks[7], (D, K), 0.2), 'k_conv_w': p(ks[8], (D, K), 0.2), 'v_conv_w': p(ks[9], (D, K), 0.2), 'g_proj_w': p(ks[10], (D, D)), 'o_norm_w': jnp.ones((D,), jnp.float32), 'o_proj_w': p(ks[11], (D, D))}
    _L0_attn_all = _L0_attn_setup()
    _L0_attn_in = {k: v for k, v in _L0_attn_all.items() if k in ('q_proj_w', 'k_proj_w', 'v_proj_w', 'b_proj_w', 'a_proj_w', 'A_log', 'dt_bias', 'q_conv_w', 'k_conv_w', 'v_conv_w', 'g_proj_w', 'o_norm_w', 'o_proj_w', )}
    del _L0_attn_all

    def _L0_ffn_setup():
        import jax, jax.numpy as jnp
        import numpy as np
        DIM = 512
        FFN_DIM = 1408
        GROUP = 128
        EPS = 1e-05

        def _quantize_weight(w, group_size):
            o, i = w.shape
            wg = w.reshape(o, i // group_size, group_size)
            scale = jnp.mean(jnp.abs(wg), axis=-1, keepdims=True) + EPS
            wq = jnp.clip(jnp.round(wg / scale), -1.0, 1.0) * scale
            return wq.reshape(o, i)

        def _bitlinear(x, w, group_size=GROUP):
            wq = w + jax.lax.stop_gradient(_quantize_weight(w, group_size) - w)
            return jnp.einsum('bsd,fd->bsf', x, wq)
        key = jax.random.key(seed)
        k_x, k_g, k_u, k_d = jax.random.split(key, 4)
        x = jax.random.normal(k_x, (8, 4096, DIM), dtype=jnp.float32)
        sd_in = 1.0 / np.sqrt(DIM)
        sd_ffn = 1.0 / np.sqrt(FFN_DIM)
        w_gate = jax.random.normal(k_g, (FFN_DIM, DIM), dtype=jnp.float32) * sd_in
        w_up = jax.random.normal(k_u, (FFN_DIM, DIM), dtype=jnp.float32) * sd_in
        w_down = jax.random.normal(k_d, (DIM, FFN_DIM), dtype=jnp.float32) * sd_ffn
        return {'x': x, 'w_gate': w_gate, 'w_up': w_up, 'w_down': w_down}
    _L0_ffn_all = _L0_ffn_setup()
    _L0_ffn_in = {k: v for k, v in _L0_ffn_all.items() if k in ('w_gate', 'w_up', 'w_down', )}
    del _L0_ffn_all

    return {
        "x": x,
        "L0_tok_sqrt_eig": _L0_tok_in["sqrt_eig"],
        "L0_tok_pct": _L0_tok_in["pct"],
        "L0_attn_q_proj_w": _L0_attn_in["q_proj_w"],
        "L0_attn_k_proj_w": _L0_attn_in["k_proj_w"],
        "L0_attn_v_proj_w": _L0_attn_in["v_proj_w"],
        "L0_attn_b_proj_w": _L0_attn_in["b_proj_w"],
        "L0_attn_a_proj_w": _L0_attn_in["a_proj_w"],
        "L0_attn_A_log": _L0_attn_in["A_log"],
        "L0_attn_dt_bias": _L0_attn_in["dt_bias"],
        "L0_attn_q_conv_w": _L0_attn_in["q_conv_w"],
        "L0_attn_k_conv_w": _L0_attn_in["k_conv_w"],
        "L0_attn_v_conv_w": _L0_attn_in["v_conv_w"],
        "L0_attn_g_proj_w": _L0_attn_in["g_proj_w"],
        "L0_attn_o_norm_w": _L0_attn_in["o_norm_w"],
        "L0_attn_o_proj_w": _L0_attn_in["o_proj_w"],
        "L0_ffn_w_gate": _L0_ffn_in["w_gate"],
        "L0_ffn_w_up": _L0_ffn_in["w_up"],
        "L0_ffn_w_down": _L0_ffn_in["w_down"],
    }

def reference(x, L0_tok_sqrt_eig, L0_tok_pct, L0_attn_q_proj_w, L0_attn_k_proj_w, L0_attn_v_proj_w, L0_attn_b_proj_w, L0_attn_a_proj_w, L0_attn_A_log, L0_attn_dt_bias, L0_attn_q_conv_w, L0_attn_k_conv_w, L0_attn_v_conv_w, L0_attn_g_proj_w, L0_attn_o_norm_w, L0_attn_o_proj_w, L0_ffn_w_gate, L0_ffn_w_up, L0_ffn_w_down):
    import jax
    import jax.numpy as jnp
    def _L0_tok_ref(xi, sqrt_eig, pct, N):
        import jax, jax.numpy as jnp
        import numpy as np
        NLAT = 256
        NLON = 2 * NLAT
        LMAX = NLAT
        MMAX = NLAT + 1
        ALPHA = 2.0
        TAU = 3.0
        SIGMA = TAU ** (0.5 * (2 * ALPHA - 2.0))
        RADIUS = 1.0

        def _legpoly(mmax, lmax, x):
            nmax = max(mmax, lmax)
            vdm = np.zeros((nmax, nmax, len(x)), dtype=np.float64)
            norm_factor = 1.0 / np.sqrt(4.0 * np.pi)
            vdm[0, 0, :] = norm_factor / np.sqrt(4.0 * np.pi)
            for l in range(1, nmax):
                vdm[l - 1, l] = np.sqrt(2 * l + 1) * x * vdm[l - 1, l - 1]
                vdm[l, l] = np.sqrt((2 * l + 1) * (1 + x) * (1 - x) / (2 * l)) * vdm[l - 1, l - 1]
            for l in range(2, nmax):
                for m in range(0, l - 1):
                    a = np.sqrt((2 * l - 1) / (l - m) * (2 * l + 1) / (l + m))
                    b = np.sqrt((l + m - 1) / (l - m) * (2 * l + 1) / (2 * l - 3) * (l - m - 1) / (l + m))
                    vdm[m, l] = x * a * vdm[m, l - 1] - b * vdm[m, l - 2]
            vdm = vdm[:mmax, :lmax]
            for m in range(1, mmax, 2):
                vdm[m] *= -1.0
            return vdm

        def _make_buffers():
            tj = np.pi * np.arange(NLAT) / (NLAT - 1)
            x = np.flip(np.cos(tj)).copy()
            pct = _legpoly(MMAX, LMAX, x).astype(np.float32)
            l = np.arange(NLAT, dtype=np.float64)
            e = SIGMA * (l * (l + 1) / RADIUS ** 2 + TAU ** 2) ** (-ALPHA / 2.0)
            se = np.tril(np.repeat(e[:, None], NLAT + 1, axis=1))
            se[0, 0] = 0.0
            sqrt_eig = se[None].astype(np.float32)
            return (jnp.asarray(pct), jnp.asarray(sqrt_eig))
        coeff = jax.lax.complex(xi[..., 0], xi[..., 1]) * sqrt_eig.astype(jnp.complex64)
        x = jnp.einsum('nlm,mlk->nkm', coeff, pct.astype(jnp.complex64))
        u = jnp.fft.irfft(x, n=NLON, axis=-1, norm='forward')
        return u

    def _L0_attn_ref(x, q_proj_w, k_proj_w, v_proj_w, b_proj_w, a_proj_w, A_log, dt_bias, q_conv_w, k_conv_w, v_conv_w, g_proj_w, o_norm_w, o_proj_w):
        import jax, jax.numpy as jnp
        import numpy as np
        EPS = 1e-05
        H = 1

        def _silu(x):
            return x * jax.nn.sigmoid(x)

        def _causal_dwconv(x, w):
            K = w.shape[1]
            xp = jnp.pad(x, ((0, 0), (K - 1, 0), (0, 0)))
            out = jax.lax.conv_general_dilated(xp.transpose(0, 2, 1), w[:, None, :], (1,), 'VALID', dimension_numbers=('NCH', 'OIH', 'NCH'), feature_group_count=w.shape[0])
            return out.transpose(0, 2, 1)

        def _l2norm(x):
            return x * jax.lax.rsqrt(jnp.sum(x * x, -1, keepdims=True) + 1e-06)

        def _gated_delta_net(x, q_proj_w, k_proj_w, v_proj_w, b_proj_w, a_proj_w, A_log, dt_bias, q_conv_w, k_conv_w, v_conv_w, g_proj_w, o_norm_w, o_proj_w):
            B, T, D = x.shape
            Dh = D // H
            scale = Dh ** (-0.5)
            q = _silu(_causal_dwconv(x @ q_proj_w.T, q_conv_w))
            k = _silu(_causal_dwconv(x @ k_proj_w.T, k_conv_w))
            v = _silu(_causal_dwconv(x @ v_proj_w.T, v_conv_w))
            beta = jax.nn.sigmoid(x @ b_proj_w.T)
            g = -jnp.exp(A_log) * jax.nn.softplus(x @ a_proj_w.T + dt_bias)
            qh = _l2norm(q.reshape(B, T, H, Dh)) * scale
            kh = _l2norm(k.reshape(B, T, H, Dh))
            vh = v.reshape(B, T, H, Dh)
            xs = (jnp.moveaxis(qh, 1, 0), jnp.moveaxis(kh, 1, 0), jnp.moveaxis(vh, 1, 0), jnp.moveaxis(g, 1, 0), jnp.moveaxis(beta, 1, 0))

            def step(S, inp):
                q_t, k_t, v_t, g_t, b_t = inp
                S = S * jnp.exp(g_t)[..., None, None]
                kv = jnp.einsum('bhk,bhkv->bhv', k_t, S)
                dv = (v_t - kv) * b_t[..., None]
                S = S + k_t[..., None] * dv[..., None, :]
                o_t = jnp.einsum('bhk,bhkv->bhv', q_t, S)
                return (S, o_t)
            S0 = jnp.zeros((B, H, Dh, Dh), x.dtype)
            _, o = jax.lax.scan(step, S0, xs)
            o = jnp.moveaxis(o, 0, 1)
            gate = (x @ g_proj_w.T).reshape(B, T, H, Dh)
            o = o * jax.lax.rsqrt(jnp.mean(o * o, -1, keepdims=True) + EPS) * o_norm_w
            o = o * _silu(gate)
            return o.reshape(B, T, D) @ o_proj_w.T
        return _gated_delta_net(x, q_proj_w, k_proj_w, v_proj_w, b_proj_w, a_proj_w, A_log, dt_bias, q_conv_w, k_conv_w, v_conv_w, g_proj_w, o_norm_w, o_proj_w)

    def _L0_ffn_ref(x, w_gate, w_up, w_down):
        import jax, jax.numpy as jnp
        import numpy as np
        DIM = 512
        FFN_DIM = 1408
        GROUP = 128
        EPS = 1e-05

        def _quantize_weight(w, group_size):
            o, i = w.shape
            wg = w.reshape(o, i // group_size, group_size)
            scale = jnp.mean(jnp.abs(wg), axis=-1, keepdims=True) + EPS
            wq = jnp.clip(jnp.round(wg / scale), -1.0, 1.0) * scale
            return wq.reshape(o, i)

        def _bitlinear(x, w, group_size=GROUP):
            wq = w + jax.lax.stop_gradient(_quantize_weight(w, group_size) - w)
            return jnp.einsum('bsd,fd->bsf', x, wq)
        gate = _bitlinear(x, w_gate)
        up = _bitlinear(x, w_up)
        h = jax.nn.silu(gate) * up
        return _bitlinear(h, w_down)

    h = _L0_tok_ref(x, L0_tok_sqrt_eig, L0_tok_pct, 32)
    h = h + _L0_attn_ref(_layernorm(h, axis=-1), L0_attn_q_proj_w, L0_attn_k_proj_w, L0_attn_v_proj_w, L0_attn_b_proj_w, L0_attn_a_proj_w, L0_attn_A_log, L0_attn_dt_bias, L0_attn_q_conv_w, L0_attn_k_conv_w, L0_attn_v_conv_w, L0_attn_g_proj_w, L0_attn_o_norm_w, L0_attn_o_proj_w)
    h = h + _L0_ffn_ref(_layernorm(h, axis=-1), L0_ffn_w_gate, L0_ffn_w_up, L0_ffn_w_down)
    return h


_drawn_inputs = setup_inputs


def setup_inputs(seed=0):
    import zlib

    import numpy as np

    out = dict(_drawn_inputs(seed))
    spreads = {'L0_attn_o_norm_w': (1.0, 0.2)}
    factors = {'L0_attn_b_proj_w': 5.927}
    for name, (base, spread) in spreads.items():
        noise = np.random.default_rng([zlib.crc32(name.encode()), seed]).standard_normal(out[name].shape)
        drawn = base * np.exp(spread * noise) if base else spread * noise
        out[name] = jnp.asarray(drawn.astype(out[name].dtype))
    for name, factor in factors.items():
        out[name] = (out[name] * factor).astype(out[name].dtype)
    return out
```

```python
from contextlib import ExitStack

import numpy as np
import concourse.bass as bass
from concourse import mybir

F32 = mybir.dt.float32
F16 = mybir.dt.float16
ALU = mybir.AluOpType
ACT = mybir.ActivationFunctionType
AX = mybir.AxisListType

P = 128
SEQS, NLAT, ORDERS = 32, 256, 257
T = NLAT
TT = T // P
D = 512
DC = D // P
FFN = 1408
FC = FFN // P
TAPS = 4
HP = P // 2
LEVELS = 7

A_UP, W_UP, H_UP = 64.0, 256.0, 16.0
UNDO_AW = 1.0 / (A_UP * W_UP)
UNDO_HW = 1.0 / (H_UP * W_UP)
LN_EPS, L2_EPS, RMS_EPS, Q_EPS = 1e-5, 1e-6, 1e-5, 1e-5

GU_COLS = 2 * DC * FFN
DN_COLS = FC * D
AT_COLS = 5 * DC * D
QUANT_COLS = GU_COLS + DN_COLS
ALL_COLS = QUANT_COLS + AT_COLS
QW = 1536
AW = 1280

MB = 64
MC = 4


def weight_phase(nc, banks, w_all, w_hi, w_lo):
    steps = [(c, QW, True) for c in range(0, QUANT_COLS, QW)] + \
            [(c, AW, False) for c in range(QUANT_COLS, ALL_COLS, AW)]
    NQ = QUANT_COLS // QW
    with ExitStack() as ctx:
        sb = lambda n, s, d=F32: ctx.enter_context(nc.sbuf_tensor(n, s, d))
        sem = lambda n: ctx.enter_context(nc.semaphore(n))
        raw = [sb(f"w_raw{i}", [P, QW]) for i in range(2)]
        mag = [sb(f"w_mag{i}", [P, QW]) for i in range(2)]
        scale = [sb(f"w_scale{i}", [P, QW]) for i in range(2)]
        below = [sb(f"w_below{i}", [P, QW]) for i in range(2)]
        ones = sb("w_ones", [P, P])
        loaded = [sem(f"w_loaded{i}") for i in range(2)]
        ones_set, mag_set, summed, scaled, above_set, below_set = map(sem, (
            "w_ones_set", "w_mag_set", "w_summed", "w_scaled", "w_above_set", "w_below_set"))
        tern, quant, delta, final, hi_set, lo_set = map(sem, (
            "w_tern", "w_quant", "w_delta", "w_final", "w_hi_set", "w_lo_set"))
        block = ctx.enter_context(nc.Block())

        @block.sync
        def _(sp):
            for n, (c, w, q) in enumerate(steps):
                if n >= 2:
                    sp.wait_ge(lo_set, n - 1)
                sp.dma_start(raw[n % 2][:, 0:w], w_all[:, c:c + w]).then_inc(loaded[n % 2], 16)

        @block.gpsimd
        def _(pool):
            nc.gpsimd.memset(ones[:, :], 1.0).then_inc(ones_set, 1)
            for n in range(NQ):
                r, m, s, b = raw[n % 2], mag[n % 2], scale[n % 2], below[n % 2]
                pool.wait_ge(below_set, n + 1)
                nc.gpsimd.tensor_tensor(m[:, :], m[:, :], b[:, :], ALU.subtract).then_inc(tern, 1)
                pool.wait_ge(tern, n + 1)
                nc.gpsimd.tensor_tensor(m[:, :], m[:, :], s[:, :], ALU.mult).then_inc(quant, 1)
                pool.wait_ge(quant, n + 1)
                nc.gpsimd.tensor_tensor(m[:, :], m[:, :], r[:, :], ALU.subtract).then_inc(delta, 1)
                pool.wait_ge(delta, n + 1)
                nc.gpsimd.tensor_tensor(r[:, :], r[:, :], m[:, :], ALU.add).then_inc(final, 1)

        @block.tensor
        def _(pe):
            pe.wait_ge(ones_set, 1)
            for n in range(NQ):
                pe.wait_ge(mag_set, n + 1)
                if n >= 2:
                    pe.wait_ge(scaled, n - 1)
                for b in range(QW // 512):
                    mm = nc.tensor.matmul(banks[3 * (n % 2) + b][:, :], ones[:, :],
                                          mag[n % 2][:, b * 512:(b + 1) * 512], start=True, stop=True)
                mm.then_inc(summed, 1)

        @block.scalar
        def _(act):
            def magnitudes(n):
                act.wait_ge(loaded[n % 2], 16 * (n // 2 + 1))
                nc.scalar.activation(mag[n % 2][:, :], raw[n % 2][:, :], ACT.Abs).then_inc(mag_set, 1)

            def high(n):
                c, w, q = steps[n]
                if q:
                    act.wait_ge(final, n + 1)
                else:
                    act.wait_ge(loaded[n % 2], 16 * (n // 2 + 1))
                nc.scalar.activation(w_hi[:, c:c + w], raw[n % 2][:, 0:w], ACT.Copy, scale=W_UP).then_inc(hi_set, 1)

            magnitudes(0)
            for n in range(len(steps)):
                if n + 1 < NQ:
                    magnitudes(n + 1)
                high(n)

        @block.vector
        def _(dve):
            def ternary(n):
                r, m, s, b = raw[n % 2], mag[n % 2], scale[n % 2], below[n % 2]
                dve.wait_ge(summed, n + 1)
                for k in range(QW // 512):
                    last = nc.vector.tensor_scalar(s[:, k * 512:(k + 1) * 512], banks[3 * (n % 2) + k][:, :],
                                                   1.0 / P, Q_EPS, ALU.mult, ALU.add)
                last.then_inc(scaled, 1)
                dve.wait_ge(scaled, n + 1)
                nc.vector.scalar_tensor_tensor(m[:, :], s[:, :], 0.5, r[:, :], ALU.mult, ALU.is_lt).then_inc(above_set, 1)
                nc.vector.scalar_tensor_tensor(b[:, :], s[:, :], -0.5, r[:, :], ALU.mult, ALU.is_gt).then_inc(below_set, 1)

            ternary(0)
            for n, (c, w, q) in enumerate(steps):
                if n + 1 < NQ:
                    ternary(n + 1)
                dve.wait_ge(hi_set, n + 1)
                nc.vector.scalar_tensor_tensor(w_lo[:, c:c + w], raw[n % 2][:, 0:w], W_UP, w_hi[:, c:c + w],
                                               ALU.mult, ALU.subtract).then_inc(lo_set, 1)


def legendre_phase(nc, banks, x, sqrt_eig, pct, z):
    J = NLAT // P
    BLOCKS = (ORDERS - 1) // MB
    LOOPS = MB // (2 * MC)
    W_X = 2 * (MB + 1)
    with ExitStack() as ctx:
        sb = lambda n, s, d=F32: ctx.enter_context(nc.sbuf_tensor(n, s, d))
        sem = lambda n: ctx.enter_context(nc.semaphore(n))
        xin = [sb(f"x_in{i}", [P, J, SEQS, W_X]) for i in range(2)]
        eig = sb("eig", [P, J, ORDERS])
        table = [sb(f"table{i}", [P, MC, J * T]) for i in range(2)]
        xs = [sb(f"x_scaled{i}", [P, J, MC, 2 * SEQS]) for i in range(2)]
        stage = [sb(f"z_stage{i}", [2 * SEQS, MC, T]) for i in range(2)]
        eig_loaded = sem("eig_loaded")
        x_loaded = [sem(f"x_loaded{i}") for i in range(2)]
        t_loaded = [sem(f"t_loaded{i}") for i in range(2)]
        x_scaled = [sem(f"x_scaled_set{i}") for i in range(2)]
        summed = [sem(f"l_summed{i}") for i in range(2)]
        copied = [sem(f"l_copied{i}") for i in range(2)]
        stored = [sem(f"l_stored{i}") for i in range(2)]
        block = ctx.enter_context(nc.Block())

        x_v = x.rearrange("n (p j) m c -> j p n (m c)", j=J)
        pct_v = pct.rearrange("m (p j) k -> p m (j k)", j=J)
        z_re = z[0:ORDERS - 1].rearrange("m n k -> n m k")
        z_im = z[ORDERS - 1:2 * (ORDERS - 1)].rearrange("m n k -> n m k")
        STEPS = BLOCKS * LOOPS

        def loop(engine, b, body):
            if b == 0:
                body(b, 0)
            with engine.Fori(1 if b == 0 else 0, LOOPS) as u:
                body(b, u)

        def wait_past(engine, semaphore, value):
            if not isinstance(value, int) or value > 0:
                engine.wait_ge(semaphore, value)

        @block.sync
        def _(sp):
            sp.dma_start(eig[:, :, :], sqrt_eig.rearrange("a (p j) m -> p (a j) m", j=J)).then_inc(eig_loaded, 16)

            def load_x(b):
                w = 2 * (MB + (b == BLOCKS - 1))
                for j in range(J):
                    sp.dma_start(xin[b % 2][:, j, :, 0:w], x_v[j, :, :, 2 * MB * b:2 * MB * b + w]).then_inc(x_loaded[b % 2], 16)

            def load_tables(b, u):
                for h in range(2):
                    m0 = u * (2 * MC) + (b * MB + h * MC)
                    m0 = m0 if isinstance(m0, int) else sp.snap(m0)
                    wait_past(sp, summed[h], u + b * LOOPS)
                    sp.dma_start(table[h][:, :, :], pct_v[:, bass.ds(m0, MC), :]).then_inc(t_loaded[h], 16)

            load_x(0)
            for b in range(BLOCKS):
                if b + 1 < BLOCKS:
                    if b >= 1:
                        for h in range(2):
                            sp.wait_ge(summed[h], b * LOOPS)
                    load_x(b + 1)
                loop(sp, b, load_tables)
            sp.wait_ge(summed[0], STEPS)
            sp.dma_start(table[0][:, 0, :], pct_v[:, ORDERS - 1, :]).then_inc(t_loaded[0], 16)

        @block.vector
        def _(dve):
            dve.wait_ge(eig_loaded, 16)

            def scale_x(b, h, m, e, n_orders):
                for j in range(J):
                    xv = xin[b % 2][:, j, :, :].rearrange("p n (m c) -> p m c n", c=2)
                    ins = nc.vector.tensor_tensor(
                        xs[h][:, j, 0:n_orders, :].rearrange("p m (c n) -> p m c n", c=2),
                        xv[:, bass.ds(m, n_orders), :, :],
                        eig[:, j, bass.ds(e, n_orders)].unsqueeze(2).unsqueeze(3).to_broadcast([P, n_orders, 2, SEQS]),
                        ALU.mult)
                ins.then_inc(x_scaled[h], 1)

            def scale_step(b, u):
                for h in range(2):
                    wait_past(dve, summed[h], u + b * LOOPS)
                    scale_x(b, h, u * (2 * MC) + h * MC, u * (2 * MC) + (b * MB + h * MC), MC)

            for b in range(BLOCKS):
                dve.wait_ge(x_loaded[b % 2], 32 * (b // 2 + 1))
                loop(dve, b, scale_step)
            dve.wait_ge(summed[0], STEPS)
            scale_x(BLOCKS - 1, 0, MB, ORDERS - 1, 1)

        @block.tensor
        def _(pe):
            def order(h, i, bank, col):
                for j in range(J):
                    mm = nc.tensor.matmul(bank[0:2 * SEQS, col:col + T], xs[h][:, j, i, :],
                                          table[h][:, i, j * T:(j + 1) * T], start=(j == 0), stop=(j == J - 1))
                return mm

            def transform(b, u):
                for h in range(2):
                    pe.wait_ge(x_scaled[h], u + (b * LOOPS + 1))
                    pe.wait_ge(t_loaded[h], u * 16 + (b * LOOPS + 1) * 16)
                    wait_past(pe, copied[h], u + b * LOOPS)
                    for i in range(MC):
                        mm = order(h, i, banks[2 * h + i // 2], (i % 2) * T)
                    mm.then_inc(summed[h], 1)

            for b in range(BLOCKS):
                loop(pe, b, transform)
            pe.wait_ge(x_scaled[0], STEPS + 1)
            pe.wait_ge(t_loaded[0], 16 * (STEPS + 1))
            pe.wait_ge(copied[0], STEPS)
            order(0, 0, banks[0], 0).then_inc(summed[0], 1)

        @block.scalar
        def _(act):
            def write_out(b, u):
                for h in range(2):
                    m0 = u * (2 * MC) + (b * MB + h * MC)
                    m0 = m0 if isinstance(m0, int) else act.snap(m0)
                    act.wait_ge(summed[h], u + (b * LOOPS + 1))
                    wait_past(act, stored[h], u * 32 + b * LOOPS * 32)
                    for k in range(2):
                        ins = nc.scalar.activation(stage[h][:, 2 * k:2 * k + 2, :].rearrange("p m k -> p (m k)"),
                                                   banks[2 * h + k][0:2 * SEQS, :], ACT.Copy)
                    ins.then_inc(copied[h], 1)
                    act.wait_ge(copied[h], u + (b * LOOPS + 1))
                    act.dma_start(z_re[:, bass.ds(m0, MC), :], stage[h][0:SEQS, :, :]).then_inc(stored[h], 16)
                    act.dma_start(z_im[:, bass.ds(m0, MC), :], stage[h][SEQS:2 * SEQS, :, :]).then_inc(stored[h], 16)

            for b in range(BLOCKS):
                loop(act, b, write_out)
            act.wait_ge(summed[0], STEPS + 1)
            for h in range(2):
                act.wait_ge(stored[h], STEPS * 32)
            nc.scalar.activation(stage[0][:, 0, :], banks[0][0:2 * SEQS, 0:T], ACT.Copy).then_inc(copied[0], 1)
            act.wait_ge(copied[0], STEPS + 1)
            act.dma_start(z[ORDERS - 1], stage[0][0:SEQS, 0, :]).then_inc(stored[0], 16)
            act.wait_ge(stored[0], STEPS * 32 + 16)


STAGES = """dft0 yt dft1 g0 u0 xt g1 e0 u1 ba k e1 q g2 u2 d0 v e2 g3 d1 norm u3 decay kk e3 d2 g4 qk t0 u4 ct1 gate0
e4 tct1 gate1 ct2 d3 tct2 vt ct3 g5 tct3 u5 d4 ct4 e5 g6 tct4 u6 d5 ct5 e6 g7 tct5 u7 d6 ct6 e7 g8 tct6 u8 w0 d7 e8
r1 g9 w1 u9 d8 o e9 g10 u10 d9 ot e10 d10 out h""".split()

STAGE_JOBS = {"xt": ["xt0", "xt1"], "k": ["k0", "k1"], "q": ["q0", "q1"], "v": ["v0", "v1"],
              "vt": ["vt0", "vt1"], "o": ["o0", "o1"], "ot": ["ot0", "ot1"], "h": ["h0", "h1"]}
FFN_STAGES = {f"{kind}{f}" for kind in "gude" for f in range(FC)} | {"yt", "out"}
ATT_JOBS = [j for st in STAGES if st not in FFN_STAGES for j in STAGE_JOBS.get(st, [st])]
BANK_OF = {j: n % 4 for n, j in enumerate(ATT_JOBS)}
BANK_OF.update({f"yt{i}": 4 + i for i in range(2)})
BANK_OF.update({f"gu{f}": 4 + f % 2 for f in range(FC)})
BANK_OF.update({f"down{t}": 6 + t for t in range(TT)})
PER_BANK = [sum(1 for b in BANK_OF.values() if b == k) for k in range(8)]
ORDINAL = {j: [i for i in BANK_OF if BANK_OF[i] == b].index(j) for j, b in BANK_OF.items()}


def sequence_phase(nc, banks, z, dft, consts, small, w_hi, w_lo, out):
    with ExitStack() as ctx:
        sb = lambda n, s, d=F32: ctx.enter_context(nc.sbuf_tensor(n, s, d))
        sem = lambda n: ctx.enter_context(nc.semaphore(n))
        dft_sb = sb("dft_sb", [P, DC, T])
        cst = sb("cst", [P, (LEVELS + 4) * P])
        ident, triu_ones, triu, low = (cst[:, 0:P], cst[:, P:3 * P], cst[:, P:2 * P], cst[:, 3 * P:4 * P])
        ones = cst[:, 2 * P:3 * P]
        masks = cst[:, 4 * P:].rearrange("p (l i) -> p l i", i=P)
        conv_w = sb("conv_w", [P, 3, DC, TAPS])
        ba_w = sb("ba_w", [P, DC, 2])
        ba_hi, ba_lo = sb("ba_hi", [P, DC, 2], F16), sb("ba_lo", [P, DC, 2], F16)
        norm_w = sb("norm_w", [P, D])
        gate_c = sb("gate_c", [P, 2])
        exps = sb("exps", [P, 2, TT])
        z_in = sb("z_in", [P, DC, T])
        odd = sb("odd", [P, TT, T])
        h = sb("h", [P, TT, D])
        xn = sb("xn", [P, TT, D])
        xt_hi, xt_lo = sb("xt_hi", [P, DC, T], F16), sb("xt_lo", [P, DC, T], F16)
        ch = {t: sb(f"ch_{t}", [P, DC, T]) for t in "kqv"}
        v_tok = sb("v_tok", [P, TT, D])
        gate = sb("gate", [P, TT, D])
        decay = sb("decay", [P, 4 * P])
        nt, pt = sb("nt", [P, 4 * P]), sb("pt", [P, 4 * P])
        gm = sb("gm", [P, 3, P])
        ct = sb("ct", [P, LEVELS, TT, P])
        inv = sb("inv", [P, 2, TT, P])
        c_t = sb("c_t", [P, LEVELS - 1, TT, P])
        w_tok = sb("w_tok", [P, TT, D])
        rhs1 = sb("rhs1", [P, D])
        h2 = sb("h2", [P, TT, D])
        yt_hi, yt_lo = sb("yt_hi", [P, DC, T], F16), sb("yt_lo", [P, DC, T], F16)
        RING = 4
        silu = sb("silu", [P, 2, T])
        hid = sb("hid", [P, 2, T])
        hid_hi, hid_lo = sb("hid_hi", [P, RING, T], F16), sb("hid_lo", [P, RING, T], F16)
        result = sb("result", [P, TT, D])
        stats = [sb(f"stats{i}", [P, TT, 6]) for i in range(2)]
        moments = [sb(f"moments{i}", [P, TT, 3]) for i in range(2)]
        mean, gap_sq, m2 = ([sb(f"{n}{i}", [P, TT]) for i in range(2)] for n in ("mean", "gap_sq", "m2"))
        var_e = [sb(f"var_e{i}", [P, TT]) for i in range(2)]
        rstd = [sb(f"rstd{i}", [P, TT]) for i in range(2)]
        zba = sb("zba", [P, TT])
        earg = sb("earg", [P, 2, TT])
        eval_ = sb("eval", [P, 2, TT])
        ln1p = sb("ln1p", [P, TT])
        beta1, beta = sb("beta1", [P, TT]), sb("beta", [P, TT])
        gpos, g = sb("gpos", [P, TT]), sb("g", [P, TT])
        ss = sb("ss", [P, 2, TT])
        rss, c_col, n_col = sb("rss", [P, TT]), sb("c_col", [P, TT]), sb("n_col", [P, TT])
        q_eps, o_ss, o_arg, o_scale = (sb(n, [P, TT]) for n in ("q_eps", "o_ss", "o_arg", "o_scale"))
        o_sq = rhs1

        gu = lambda w, which: w[:, 0:GU_COLS].rearrange("p (t c f) -> p t c f", t=2, c=DC)[:, which]
        dn = lambda w: w[:, GU_COLS:QUANT_COLS].rearrange("p (c o) -> p c o", c=FC)
        at = lambda w, which: w[:, QUANT_COLS:].rearrange("p (t c o) -> p t c o", t=5, c=DC)[:, "qkvgo".index(which)]

        filled = [sem(f"bank_filled{b}") for b in range(8)]
        emptied = [sem(f"bank_emptied{b}") for b in range(8)]
        PER = dict(z_loaded=32, odd=TT, result_free=32, stats=TT, moments=2, mean=1, gap_sq=1, m2=1, var_e=1, rstd=1, xn=TT, xt_hi=2,
                   ba_a=1, ba_exp=1, ba_ln=1, beta1=1, beta=1, gpos=1, g=1, gm=3,
                   tap1=12, taps=30, silu_k=1, silu_q=1, silu_v=1, sq_k=1, sq_q=1, gate_w=1,
                   rss=1, c_col=1, n_col=1, q_eps=1, decay_set=1, ct=LEVELS, s0=1,
                   o_ss=2, o_arg=1, o_scale=1, og_hi=2,
                   stats2=TT, moments2=2, mean2=1, gap_sq2=1, m22=1, var_e2=1, rstd2=1, yn=TT, yt_hi=2,
                   silu=FC, hid_hi=FC, hid_lo=FC)
        sems = {n: sem(n) for n in PER}

        def level_cols(ap, lv, odd_blocks):
            if len(ap.shape) == 2:
                return ap.rearrange("p (b e i) -> p e b i", e=2, i=1 << lv)[:, odd_blocks]
            return ap.rearrange("p t (b e i) -> p e t b i", e=2, i=1 << lv)[:, odd_blocks]

        def after(eng, step, s, k=None):
            v = s * PER[step] + (PER[step] if k is None else k)
            if not isinstance(v, int) or v > 0:
                eng.wait_ge(sems[step], v)

        def job_filled(eng, job, s):
            b = BANK_OF[job]
            eng.wait_ge(filled[b], s * PER_BANK[b] + ORDINAL[job] + 1)

        def job_emptied(eng, job, s):
            b = BANK_OF[job]
            eng.wait_ge(emptied[b], s * PER_BANK[b] + ORDINAL[job] + 1)

        def bank_free(eng, job, s):
            b = BANK_OF[job]
            v = s * PER_BANK[b] + ORDINAL[job]
            if not isinstance(v, int) or v > 0:
                eng.wait_ge(emptied[b], v)

        def bank(job):
            return banks[BANK_OF[job]]

        def earlier(s):
            return not isinstance(s, int) or s > 0

        const_loaded, setup_act, setup_dve = sem("const_loaded"), sem("setup_act"), sem("setup_dve")
        setup_pool = sem("setup_pool")
        z_v = z.rearrange("(w r e) n k -> n e r w k", w=2, e=2)

        def run(engine, body):
            body(0, None)
            with engine.Fori(1, SEQS) as s:
                body(s, s - 1)
            body(None, SEQS - 1)

        block = ctx.enter_context(nc.Block())

        @block.sync
        def _(sp):
            for dst, src in ((dft_sb, dft.rearrange("(c r) j -> r c j", c=DC)), (cst, consts), (conv_w, small["conv"]),
                             (ba_w, small["ba"]), (norm_w, small["norm"]), (gate_c, small["gate"])):
                sp.dma_start(dst[:], src).then_inc(const_loaded, 16)
            def load_z(n):
                for e in range(2):
                    sp.dma_start(z_in[:, 2 * e:2 * e + 2, :], z_v[n, e]).then_inc(sems["z_loaded"], 16)

            load_z(0)

            def body(s, r):
                if s is not None and not (isinstance(s, int) and s == SEQS - 1):
                    nxt = s + 1 if isinstance(s, int) else sp.snap(s + 1)
                    job_filled(sp, "dft1", s)
                    load_z(nxt)
                if r is not None:
                    rr = r if isinstance(r, int) else sp.snap(r)
                    for t in range(TT):
                        job_emptied(sp, f"down{t}", r)
                        sp.dma_start(out[rr, t * P:(t + 1) * P, :], result[:, t, :]).then_inc(sems["result_free"], 16)

            body(0, None)
            with sp.Fori(1, SEQS - 1) as s:
                body(s, s - 1)
            body(SEQS - 1, SEQS - 2)
            body(None, SEQS - 1)
            after(sp, "result_free", SEQS - 1, 33)

        @block.tensor
        def _(pe):
            pe.wait_ge(const_loaded, 6 * 16)
            pe.wait_ge(setup_dve, 3)

            def pairs(out_ap, lhs, rhs, cols_l, cols_r, chunks, opened=True, closed=True):
                n = 0
                for c in range(chunks):
                    for a, b in ((0, 0), (0, 1), (1, 0)):
                        mm = nc.tensor.matmul(out_ap, lhs[a][:, c, cols_l], rhs[b][:, c, cols_r],
                                              start=opened and n == 0, stop=closed and n == 3 * chunks - 1)
                        n += 1
                return mm

            XT, YT = (xt_hi, xt_lo), (yt_hi, yt_lo)
            sl = lambda a, n: slice(a, a + n)

            def full(job):
                return filled[BANK_OF[job]]

            def dft(t, s):
                after(pe, "z_loaded", s)
                bank_free(pe, f"dft{t}", s)
                for e in range(2):
                    for c in range(2 * e, 2 * e + 2):
                        mm = nc.tensor.matmul(bank(f"dft{t}")[:, sl(e * T, T)], z_in[:, c, sl(t * P, P)],
                                              dft_sb[:, c, :], start=(c == 2 * e), stop=(c == 2 * e + 1))
                mm.then_inc(full(f"dft{t}"), 1)

            def transposes(kind, src, s):
                for half in range(2):
                    job = f"{kind}{half}"
                    if kind != "yt":
                        bank_free(pe, job, s)
                    for cc in range(2):
                        for t in range(TT):
                            mm = nc.tensor.transpose(bank(job)[:, sl(cc * T + t * P, P)],
                                                     src[:, t, sl((2 * half + cc) * P, P)], ident)
                    mm.then_inc(full(job), 1)

            def xt(s):
                after(pe, "xn", s)
                transposes("xt", xn, s)

            def ba(s):
                job_emptied(pe, "xt1", s)
                bank_free(pe, "ba", s)
                for t in range(TT):
                    mm = pairs(bank("ba")[:, sl(2 * t, 2)], XT, (ba_hi, ba_lo), sl(t * P, P), slice(None), DC)
                mm.then_inc(full("ba"), 1)

            def channels(which, s):
                w = (at(w_hi, which), at(w_lo, which))
                for i in range(2):
                    job = f"{which}{i}"
                    bank_free(pe, job, s)
                    for oc in range(2):
                        mm = pairs(bank(job)[:, sl(oc * T, T)], w, XT, sl((2 * i + oc) * P, P), slice(None), DC)
                    mm.then_inc(full(job), 1)

            def gate_job(t, s):
                job = f"gate{t}"
                bank_free(pe, job, s)
                w = (at(w_hi, "g"), at(w_lo, "g"))
                pairs(bank(job)[:, :], XT, w, sl(t * P, P), slice(None), DC).then_inc(full(job), 1)

            def norm(s):
                bank_free(pe, "norm", s)
                for n, (buf, step) in enumerate(((xn, "sq_q"), (w_tok, "sq_k"))):
                    after(pe, step, s)
                    sq = buf[:, :, :].rearrange("p t (c x) -> p (t c) x", x=T)
                    for t in range(TT):
                        for c in range(DC):
                            mm = nc.tensor.matmul(bank("norm")[:, 2 * n + t:2 * n + t + 1], sq[:, c, sl(t * P, P)],
                                                  ones[:, 0:1], start=(c == 0), stop=(c == DC - 1))
                mm.then_inc(full("norm"), 1)

            def decay_job(s):
                after(pe, "gm", s)
                bank_free(pe, "decay", s)
                b = bank("decay")
                nc.tensor.matmul(b[:, 0:2 * P], gm[:, 0, :], triu_ones, start=True, stop=False)
                nc.tensor.matmul(b[:, P:2 * P], gm[:, 2, :], triu, start=False, stop=True)
                nc.tensor.matmul(b[:, 2 * P:3 * P], gm[:, 1, :], triu, start=True, stop=True).then_inc(full("decay"), 1)

            def gram(job, which, s):
                after(pe, "silu_k", s)
                after(pe, f"silu_{which}", s)
                bank_free(pe, job, s)
                for cols, j0, n in ((0, 0, 2 * P), (2 * P, P, P)):
                    for c in range(DC):
                        mm = nc.tensor.matmul(bank(job)[:, sl(cols, n)], ch["k"][:, c, sl(j0, P)],
                                              ch[which][:, c, sl(j0, n)], start=(c == 0), stop=(c == DC - 1))
                mm.then_inc(full(job), 1)

            def t0(s):
                after(pe, "s0", s)
                bank_free(pe, "t0", s)
                for t in range(TT):
                    mm = nc.tensor.transpose(bank("t0")[:, sl(t * P, P)], inv[:, 1, t, :], ident)
                mm.then_inc(full("t0"), 1)

            def vt(s):
                after(pe, "silu_v", s)
                for t in range(TT):
                    job = f"vt{t}"
                    bank_free(pe, job, s)
                    for c in range(DC):
                        mm = nc.tensor.transpose(bank(job)[:, sl(c * P, P)], ch["v"][:, c, sl(t * P, P)], ident)
                    mm.then_inc(full(job), 1)

            def ct_job(lv, s):
                job_emptied(pe, "t0" if lv == 1 else f"tct{lv - 1}", s)
                after(pe, "ct", s)
                bank_free(pe, f"ct{lv}", s)
                for t in range(TT):
                    mm = nc.tensor.matmul(bank(f"ct{lv}")[:, sl(t * HP, HP)], ct[:, lv, t, :],
                                          level_cols(inv[:, 0, t, :], lv, 0), start=True, stop=True)
                mm.then_inc(full(f"ct{lv}"), 1)

            def tct_job(lv, s):
                job_emptied(pe, f"ct{lv}", s)
                bank_free(pe, f"tct{lv}", s)
                b = bank(f"tct{lv}")
                for t in range(TT):
                    if lv < LEVELS - 1:
                        nc.tensor.matmul(b[:, sl(t * HP, HP)], inv[:, 1, t, :], level_cols(c_t[:, lv - 1, t, :], lv, 0),
                                         start=True, stop=True)
                    mm = nc.tensor.matmul(b[:, sl((2 + t) * HP, HP)], c_t[:, lv - 1, t, :],
                                          level_cols(inv[:, 1, t, :], lv, 1), start=True, stop=True)
                mm.then_inc(full(f"tct{lv}"), 1)

            def w0(s):
                job_emptied(pe, f"tct{LEVELS - 1}", s)
                job_emptied(pe, "vt0", s)
                bank_free(pe, "w0", s)
                nc.tensor.matmul(bank("w0")[:, :], inv[:, 1, 0, :], v_tok[:, 0, :], start=True, stop=True).then_inc(full("w0"), 1)

            def r1(s):
                job_emptied(pe, "w0", s)
                bank_free(pe, "r1", s)
                nc.tensor.matmul(bank("r1")[:, :], nt[:, P:2 * P], w_tok[:, 0, :], start=True, stop=True).then_inc(full("r1"), 1)

            def w1(s):
                job_emptied(pe, "r1", s)
                bank_free(pe, "w1", s)
                nc.tensor.matmul(bank("w1")[:, :], inv[:, 1, 1, :], rhs1[:, :], start=True, stop=True).then_inc(full("w1"), 1)

            def o(s):
                job_emptied(pe, "qk", s)
                bank_free(pe, "o0", s)
                nc.tensor.matmul(bank("o0")[:, :], pt[:, 0:P], w_tok[:, 0, :], start=True, stop=True).then_inc(full("o0"), 1)
                job_emptied(pe, "w1", s)
                bank_free(pe, "o1", s)
                nc.tensor.matmul(bank("o1")[:, :], pt[:, P:2 * P], w_tok[:, 0, :], start=True, stop=False)
                nc.tensor.matmul(bank("o1")[:, :], pt[:, 2 * P:3 * P], w_tok[:, 1, :], start=False, stop=True).then_inc(full("o1"), 1)

            def ot(s):
                job_emptied(pe, "o1", s)
                transposes("ot", v_tok, s)

            def h_job(s):
                job_emptied(pe, "ot1", s)
                w = (at(w_hi, "o"), at(w_lo, "o"))
                for t in range(TT):
                    job = f"h{t}"
                    bank_free(pe, job, s)
                    pairs(bank(job)[:, :], XT, w, sl(t * P, P), slice(None), DC).then_inc(full(job), 1)

            def yt(r):
                after(pe, "yn", r)
                transposes("yt", xn, r)

            def g_half(f, r):
                if f == 0:
                    job_emptied(pe, "yt1", r)
                bank_free(pe, f"gu{f}", r)
                pairs(bank(f"gu{f}")[:, 0:T], (gu(w_hi, 0), gu(w_lo, 0)), YT, sl(f * P, P), slice(None), DC)

            def u_half(f, r):
                pairs(bank(f"gu{f}")[:, T:2 * T], (gu(w_hi, 1), gu(w_lo, 1)), YT, sl(f * P, P), slice(None), DC)\
                    .then_inc(full(f"gu{f}"), 1)

            def d(f, r):
                after(pe, "hid_lo", r, f + 1)
                for t in range(TT):
                    job = f"down{t}"
                    for n, (a, b) in enumerate(((hid_hi, w_hi), (hid_hi, w_lo), (hid_lo, w_hi))):
                        mm = nc.tensor.matmul(bank(job)[:, :], a[:, f % RING, sl(t * P, P)], dn(b)[:, f, :],
                                              start=(f == 0 and n == 0), stop=(f == FC - 1 and n == 2))
                    if f == FC - 1:
                        mm.then_inc(full(job), 1)

            att = dict(dft0=lambda s: dft(0, s), dft1=lambda s: dft(1, s), xt=xt, ba=ba, k=lambda s: channels("k", s), q=lambda s: channels("q", s),
                       v=lambda s: channels("v", s), norm=norm, decay=decay_job, kk=lambda s: gram("kk", "k", s),
                       qk=lambda s: gram("qk", "q", s), gate0=lambda s: gate_job(0, s), gate1=lambda s: gate_job(1, s),
                       t0=t0, vt=vt, w0=w0, r1=r1, w1=w1, o=o, ot=ot, h=h_job)

            def body(s, r):
                for stage in STAGES:
                    if stage in att:
                        if s is not None:
                            att[stage](s)
                    elif stage[:2] == "ct" or stage[:3] == "tct":
                        if s is not None:
                            (ct_job if stage[0] == "c" else tct_job)(int(stage[-1]), s)
                    elif stage == "yt" and r is not None:
                        yt(r)
                    elif r is not None and stage != "out":
                        {"g": g_half, "u": u_half, "d": d, "e": lambda f, r: None}[stage[0]](int(stage[1:]), r)

            run(pe, body)

        @block.scalar
        def _(act):
            act.wait_ge(const_loaded, 6 * 16)
            nc.scalar.activation(gate_c[:, 0:1], gate_c[:, 0:1], ACT.Exp).then_inc(setup_act, 1)
            nc.scalar.activation(ba_hi[:, :, :], ba_w[:, :, :], ACT.Copy, scale=W_UP).then_inc(setup_act, 1)
            act.wait_ge(setup_dve, 3)

            def empty(job):
                return emptied[BANK_OF[job]]

            def dft(t, s):
                if earlier(s):
                    job_emptied(act, "h1", s - 1)
                job_filled(act, f"dft{t}", s)
                nc.scalar.activation(odd[:, t, :], bank(f"dft{t}")[:, T:2 * T], ACT.Copy).then_inc(sems["odd"], 1)

            def halves(kind, dst, step, up, s):
                for i in range(2):
                    job_filled(act, f"{kind}{i}", s)
                    nc.scalar.activation(dst[:, 2 * i:2 * i + 2, :].rearrange("p c x -> p (c x)"),
                                         bank(f"{kind}{i}")[:, :], ACT.Copy, scale=up).then_inc(sems[step], 1)

            def xt(s):
                if earlier(s):
                    job_filled(act, "h1", s - 1)
                halves("xt", xt_hi, "xt_hi", 1.0, s)

            def ba(s):
                after(act, "ba_a", s)
                nc.scalar.activation(eval_[:, :, :], earg[:, :, :], ACT.Exp).then_inc(sems["ba_exp"], 1)
                after(act, "ba_exp", s)
                nc.scalar.activation(ln1p[:, :], eval_[:, 1, :], ACT.Ln, bias=1.0).then_inc(sems["ba_ln"], 1)

            def taps(which, s):
                for i in range(2):
                    job_filled(act, f"{which}{i}", s)
                    for oc in range(2):
                        c = 2 * i + oc
                        nc.scalar.activation(ch[which][:, c, :], bank(f"{which}{i}")[:, oc * T:(oc + 1) * T], ACT.Copy,
                                             scale=conv_w[:, "qkv".index(which), c, TAPS - 1:TAPS]).then_inc(sems["tap1"], 1)

            def swish(which, s):
                job_emptied(act, f"{which}1", s)
                flat = ch[which][:, :, :].rearrange("p c x -> p (c x)")
                nc.scalar.activation(flat, flat, ACT.Silu).then_inc(sems[f"silu_{which}"], 1)

            def square(which, buf, s):
                after(act, f"silu_{which}", s)
                nc.scalar.activation(buf[:, :, :].rearrange("p t x -> p (t x)"),
                                     ch[which][:, :, :].rearrange("p c x -> p (c x)"),
                                     ACT.Square).then_inc(sems[f"sq_{which}"], 1)

            def q(s):
                taps("q", s)
                swish("k", s)
                square("k", w_tok, s)

            def v(s):
                taps("v", s)
                swish("q", s)
                square("q", xn, s)

            def decay_exp(s):
                job_filled(act, "decay", s)
                nc.scalar.activation(decay[:, 0:3 * P], bank("decay")[:, 0:3 * P], ACT.Exp).then_inc(empty("decay"), 1)

            def gate_half(t, s):
                job_filled(act, f"gate{t}", s)
                nc.scalar.activation(gate[:, t, :], bank(f"gate{t}")[:, :], ACT.Silu, scale=UNDO_AW).then_inc(empty(f"gate{t}"), 1)

            def t0(s):
                job_filled(act, "t0", s)
                nc.scalar.activation(inv[:, 0, :, :].rearrange("p t x -> p (t x)"), bank("t0")[:, 0:TT * P],
                                     ACT.Copy).then_inc(empty("t0"), 1)

            def vt(s):
                after(act, "n_col", s)
                for t in range(TT):
                    job_filled(act, f"vt{t}", s)
                    nc.scalar.activation(v_tok[:, t, :], bank(f"vt{t}")[:, :], ACT.Copy,
                                         scale=n_col[:, t:t + 1]).then_inc(empty(f"vt{t}"), 1)

            def ct_copy(lv, s):
                job_filled(act, f"ct{lv}", s)
                nc.scalar.activation(level_cols(c_t[:, lv - 1, :, :], lv, 0),
                                     bank(f"ct{lv}")[:, 0:P].rearrange("p (t b i) -> p t b i", t=TT, i=1 << lv),
                                     ACT.Copy).then_inc(empty(f"ct{lv}"), 1)

            def w_copy(t, s):
                job_filled(act, f"w{t}", s)
                nc.scalar.activation(w_tok[:, t, :], bank(f"w{t}")[:, :], ACT.Copy).then_inc(empty(f"w{t}"), 1)

            def o(s):
                for t in range(TT):
                    job_filled(act, f"o{t}", s)
                    if t:
                        after(act, "o_ss", s, t)
                    nc.scalar.activation(o_sq[:, :], bank(f"o{t}")[:, :], ACT.Square,
                                         accum_out=o_ss[:, t:t + 1]).then_inc(sems["o_ss"], 1)

            def silu_f(f, r):
                job_filled(act, f"gu{f}", r)
                nc.scalar.activation(silu[:, f % 2, :], bank(f"gu{f}")[:, 0:T], ACT.Silu, scale=UNDO_AW).then_inc(sems["silu"], 1)

            def hid_high(f, r):
                job_emptied(act, f"gu{f}", r)
                nc.scalar.activation(hid_hi[:, f % RING, :], hid[:, f % 2, :], ACT.Copy).then_inc(sems["hid_hi"], 1)

            att = dict(dft0=lambda s: dft(0, s), dft1=lambda s: dft(1, s), xt=xt, ba=ba, k=lambda s: taps("k", s), q=q, v=v, norm=lambda s: swish("v", s),
                       decay=decay_exp, gate0=lambda s: gate_half(0, s), gate1=lambda s: gate_half(1, s), t0=t0, vt=vt,
                       w0=lambda s: w_copy(0, s), w1=lambda s: w_copy(1, s), o=o,
                       ot=lambda s: halves("ot", xt_hi, "og_hi", A_UP, s))

            def body(s, r):
                for stage in STAGES:
                    if stage in att and s is not None:
                        att[stage](s)
                    elif stage == "yt" and r is not None:
                        halves("yt", yt_hi, "yt_hi", 1.0, r)
                    elif stage[:2] == "ct" and s is not None:
                        ct_copy(int(stage[-1]), s)
                    elif stage[0] == "u" and r is not None:
                        silu_f(int(stage[1:]), r)
                    elif stage[0] == "e" and r is not None:
                        hid_high(int(stage[1:]), r)

            run(act, body)

        @block.gpsimd
        def _(pool):
            nc.gpsimd.memset(c_t[:, :, :, :], 0.0).then_inc(setup_pool, 1)
            nc.gpsimd.memset(exps[:, 0, :], -0.5).then_inc(setup_pool, 1)
            nc.gpsimd.memset(exps[:, 1, :], 0.5).then_inc(setup_pool, 1)
            pool.wait_ge(setup_pool, 3)
            pool.wait_ge(const_loaded, 6 * 16)

            def power(dst, src, which, step_in, step_out, s):
                if step_in in BANK_OF:
                    job_emptied(pool, step_in, s)
                else:
                    after(pool, step_in, s)
                nc.gpsimd.tensor_tensor(dst, src, exps[:, which, :], ALU.pow).then_inc(sems[step_out], 1)

            diag = lambda buf: buf[:, :].rearrange("p (t x) -> p t x", t=TT)[:, :, 0:P]

            def decay_mask(s):
                job_emptied(pool, "decay", s)
                nc.gpsimd.tensor_tensor(diag(decay), diag(decay), triu.unsqueeze(1).to_broadcast([P, TT, P]),
                                        ALU.mult).then_inc(sems["decay_set"], 1)

            def level_blocks(s):
                job_emptied(pool, "kk", s)
                for lv in range(LEVELS):
                    nc.gpsimd.tensor_tensor(ct[:, lv, :, :], diag(nt), masks[:, lv, :].unsqueeze(1).to_broadcast([P, TT, P]),
                                            ALU.mult).then_inc(sems["ct"], 1)

            def gate_norm(s):
                job_emptied(pool, "gate0", s)
                job_emptied(pool, "gate1", s)
                nc.gpsimd.tensor_tensor(gate[:, :, :], gate[:, :, :], norm_w[:, :].unsqueeze(1).to_broadcast([P, TT, D]),
                                        ALU.mult).then_inc(sems["gate_w"], 1)

            def hid_low(f, r):
                after(pool, "hid_hi", r, f + 1)
                nc.gpsimd.tensor_tensor(hid_lo[:, f % RING, :], hid[:, f % 2, :], hid_hi[:, f % RING, :],
                                        ALU.subtract).then_inc(sems["hid_lo"], 1)

            att = dict(dft1=lambda s: power(rstd[0][:, :], var_e[0][:, :], 0, "var_e", "rstd", s),
                       norm=lambda s: power(n_col[:, :], ss[:, 1, :], 1, "norm", "n_col", s),
                       decay=decay_mask, kk=level_blocks, gate1=gate_norm,
                       o=lambda s: power(o_scale[:, :], o_arg[:, :], 0, "o_arg", "o_scale", s),
                       h=lambda s: power(rstd[1][:, :], var_e[1][:, :], 0, "var_e2", "rstd2", s))

            def body(s, r):
                for stage in STAGES:
                    if stage in att and s is not None:
                        att[stage](s)
                    elif stage[0] == "e" and r is not None:
                        hid_low(int(stage[1:]), r)

            run(pool, body)

        @block.vector
        def _(dve):
            dve.wait_ge(const_loaded, 6 * 16)
            dve.wait_ge(setup_act, 2)
            nc.vector.tensor_scalar(gate_c[:, 0:1], gate_c[:, 0:1], -1.0, None, ALU.mult).then_inc(setup_dve, 1)
            nc.vector.tensor_scalar(conv_w[:, :, :, :].rearrange("p a b c -> p (a b c)"),
                                    conv_w[:, :, :, :].rearrange("p a b c -> p (a b c)"), UNDO_AW, None,
                                    ALU.mult).then_inc(setup_dve, 1)
            nc.vector.scalar_tensor_tensor(ba_lo[:, :, :], ba_w[:, :, :], W_UP, ba_hi[:, :, :], ALU.mult,
                                           ALU.subtract).then_inc(setup_dve, 1)
            dve.wait_ge(setup_dve, 3)
            nc.vector.memset(result[:, :, 0:2], 0.0).then_inc(sems["result_free"], 1)

            def empty(job):
                return emptied[BANK_OF[job]]

            def layer_norm(src, src_ready, k, names, dst_free, s):
                n_stats, n_mom, n_mean, n_sq, n_m2, n_var, n_rstd, n_out = names
                for t in range(TT):
                    src_ready(t)
                    nc.vector.bn_stats(stats[k][:, t, :], src[:, t, :]).then_inc(sems[n_stats], 1)
                after(dve, n_stats, s)
                nc.vector.tensor_tensor(moments[k][:, :, 0:2], stats[k][:, :, 1:3], stats[k][:, :, 4:6],
                                        ALU.add).then_inc(sems[n_mom], 1)
                nc.vector.tensor_tensor(moments[k][:, :, 2], stats[k][:, :, 1], stats[k][:, :, 4],
                                        ALU.subtract).then_inc(sems[n_mom], 1)
                after(dve, n_mom, s)
                nc.vector.tensor_scalar(mean[k][:, :], moments[k][:, :, 0], 0.5, None, ALU.mult).then_inc(sems[n_mean], 1)
                nc.vector.scalar_tensor_tensor(gap_sq[k][:, :], moments[k][:, :, 2], D / 4.0, moments[k][:, :, 2], ALU.mult,
                                               ALU.mult).then_inc(sems[n_sq], 1)
                after(dve, n_sq, s)
                nc.vector.tensor_tensor(m2[k][:, :], gap_sq[k][:, :], moments[k][:, :, 1], ALU.add).then_inc(sems[n_m2], 1)
                after(dve, n_m2, s)
                nc.vector.tensor_scalar(var_e[k][:, :], m2[k][:, :], 1.0 / (D * A_UP ** 2), LN_EPS / A_UP ** 2, ALU.mult,
                                        ALU.add).then_inc(sems[n_var], 1)
                dst_free()
                after(dve, n_rstd, s)
                for t in range(TT):
                    nc.vector.tensor_scalar(xn[:, t, :], src[:, t, :], mean[k][:, t:t + 1], rstd[k][:, t:t + 1],
                                            ALU.subtract, ALU.mult).then_inc(sems[n_out], 1)

            def halves_joined(t, s):
                if earlier(s):
                    job_emptied(dve, "h1", s - 1)
                after(dve, "odd", s, t + 1)
                job_filled(dve, f"dft{t}", s)
                even = bank(f"dft{t}")[:, 0:T]
                nc.vector.tensor_tensor(h[:, t, 0:T], even, odd[:, t, :], ALU.add)
                nc.vector.tensor_tensor(h[:, t, T:2 * T], even, odd[:, t, :], ALU.subtract).then_inc(empty(f"dft{t}"), 1)

            def dft(s):
                halves_joined(1, s)
                layer_norm(h, lambda t: job_emptied(dve, f"dft{t}", s), 0, ("stats", "moments", "mean", "gap_sq", "m2", "var_e", "rstd", "xn"),
                           lambda: earlier(s) and job_filled(dve, "yt1", s - 1), s)

            def lows(kind, dst, hi, step, up, s):
                for i in range(2):
                    after(dve, step, s, i + 1)
                    job_filled(dve, f"{kind}{i}", s)
                    view = lambda b: b[:, 2 * i:2 * i + 2, :].rearrange("p c x -> p (c x)")
                    nc.vector.scalar_tensor_tensor(view(dst), bank(f"{kind}{i}")[:, :], up, view(hi), ALU.mult,
                                                   ALU.subtract).then_inc(empty(f"{kind}{i}"), 1)

            def ba(s):
                job_filled(dve, "ba", s)
                zb = bank("ba")[:, 0:2 * TT].rearrange("p (t w) -> p w t", w=2)
                nc.vector.tensor_scalar(earg[:, 0, :], zb[:, 0, :], -UNDO_AW, None, ALU.mult)
                nc.vector.tensor_scalar(zba[:, :], zb[:, 1, :], UNDO_AW, gate_c[:, 1:2], ALU.mult,
                                        ALU.add).then_inc(empty("ba"), 1)
                job_emptied(dve, "ba", s)
                nc.vector.scalar_tensor_tensor(earg[:, 1, :], zba[:, :], -1.0, zba[:, :], ALU.mult,
                                               ALU.min).then_inc(sems["ba_a"], 1)
                after(dve, "ba_ln", s)
                nc.vector.tensor_scalar(beta1[:, :], eval_[:, 0, :], 1.0, None, ALU.add).then_inc(sems["beta1"], 1)
                nc.vector.scalar_tensor_tensor(gpos[:, :], zba[:, :], 0.0, ln1p[:, :], ALU.max,
                                               ALU.add).then_inc(sems["gpos"], 1)
                after(dve, "beta1", s)
                nc.vector.reciprocal(beta[:, :], beta1[:, :]).then_inc(sems["beta"], 1)
                after(dve, "gpos", s)
                nc.vector.tensor_scalar(g[:, :], gpos[:, :], gate_c[:, 0:1], None, ALU.mult).then_inc(sems["g"], 1)
                after(dve, "g", s)
                for n, (m, t) in enumerate(((low, 0), (low, 1), (ones, 1))):
                    nc.vector.tensor_scalar(gm[:, n, :], m, g[:, t:t + 1], None, ALU.mult).then_inc(sems["gm"], 1)

            def taps(which, s):
                base = "kqv".index(which)
                for i in range(2):
                    job = f"{which}{i}"
                    for tap in range(1, TAPS):
                        for oc in range(2):
                            c = 2 * i + oc
                            if tap == 1 and oc == 0:
                                after(dve, "tap1", s, 4 * base + 2 * i + 2)
                                job_filled(dve, job, s)
                            elif tap > 1:
                                after(dve, "taps", s, 10 * base + 5 * i + 2 * (tap - 2) + oc + 1)
                            dst = ch[which][:, c, tap:T]
                            ins = nc.vector.scalar_tensor_tensor(
                                dst, bank(job)[:, oc * T:(oc + 1) * T - tap],
                                conv_w[:, "qkv".index(which), c, TAPS - 1 - tap:TAPS - tap], dst, ALU.mult, ALU.add)
                            if tap < TAPS - 1 or oc == 0:
                                ins.then_inc(sems["taps"], 1)
                            else:
                                ins.then_inc(empty(job), 1)

            def norm(s):
                job_filled(dve, "norm", s)
                nc.vector.tensor_scalar(ss[:, :, :].rearrange("p w t -> p (w t)"), bank("norm")[:, 0:2 * TT], L2_EPS, None,
                                        ALU.add).then_inc(empty("norm"), 1)
                job_emptied(dve, "norm", s)
                nc.vector.reciprocal(rss[:, :], ss[:, 1, :]).then_inc(sems["rss"], 1)
                nc.vector.tensor_scalar(q_eps[:, :], ss[:, 0, :], RMS_EPS * D, None, ALU.mult).then_inc(sems["q_eps"], 1)
                after(dve, "rss", s)
                nc.vector.tensor_tensor(c_col[:, :], beta[:, :], rss[:, :], ALU.mult).then_inc(sems["c_col"], 1)

            def gram(job, dst, s):
                job_filled(dve, job, s)
                after(dve, "decay_set", s)
                after(dve, "c_col", s)
                nc.vector.scalar_tensor_tensor(dst[:, 0:2 * P], bank(job)[:, 0:2 * P], c_col[:, 0:1], decay[:, 0:2 * P],
                                               ALU.mult, ALU.mult)
                nc.vector.scalar_tensor_tensor(dst[:, 2 * P:3 * P], bank(job)[:, 2 * P:3 * P], c_col[:, 1:2],
                                               decay[:, 2 * P:3 * P], ALU.mult, ALU.mult).then_inc(empty(job), 1)

            def t0(s):
                after(dve, "ct", s, 1)
                nc.vector.tensor_tensor(inv[:, 1, :, :], ident.unsqueeze(1).to_broadcast([P, TT, P]), ct[:, 0, :, :],
                                        ALU.subtract).then_inc(sems["s0"], 1)

            def merge(lv, s):
                job_filled(dve, f"tct{lv}", s)
                for side in range(0 if lv < LEVELS - 1 else 1, 2):
                    view = level_cols(inv[:, side, :, :], lv, side)
                    ins = nc.vector.tensor_tensor(view, view, bank(f"tct{lv}")[:, side * P:(side + 1) * P].rearrange(
                        "p (t b i) -> p t b i", t=TT, i=1 << lv), ALU.subtract)
                ins.then_inc(empty(f"tct{lv}"), 1)

            def r1(s):
                job_filled(dve, "r1", s)
                job_emptied(dve, "vt1", s)
                nc.vector.tensor_tensor(rhs1[:, :], v_tok[:, 1, :], bank("r1")[:, :], ALU.subtract).then_inc(empty("r1"), 1)

            def o(s):
                after(dve, "o_ss", s)
                nc.vector.scalar_tensor_tensor(o_arg[:, :], o_ss[:, :], 1.0 / D, q_eps[:, :], ALU.mult,
                                               ALU.add).then_inc(sems["o_arg"], 1)
                after(dve, "o_scale", s)
                after(dve, "gate_w", s)
                for t in range(TT):
                    job_filled(dve, f"o{t}", s)
                    nc.vector.scalar_tensor_tensor(v_tok[:, t, :], bank(f"o{t}")[:, :], o_scale[:, t:t + 1], gate[:, t, :],
                                                   ALU.mult, ALU.mult).then_inc(empty(f"o{t}"), 1)

            def h_add(s):
                for t in range(TT):
                    job_filled(dve, f"h{t}", s)
                    if earlier(s):
                        job_emptied(dve, f"down{t}", s - 1)
                    nc.vector.scalar_tensor_tensor(h2[:, t, :], bank(f"h{t}")[:, :], UNDO_AW, h[:, t, :], ALU.mult,
                                                   ALU.add).then_inc(empty(f"h{t}"), 1)
                layer_norm(h2, lambda t: job_emptied(dve, f"h{t}", s), 1, ("stats2", "moments2", "mean2", "gap_sq2", "m22", "var_e2", "rstd2", "yn"),
                           lambda: None, s)

            def hidden(f, r):
                after(dve, "silu", r, f + 1)
                if f >= 2:
                    after(dve, "hid_lo", r, f - 1)
                nc.vector.scalar_tensor_tensor(hid[:, f % 2, :], bank(f"gu{f}")[:, T:2 * T], UNDO_AW * H_UP,
                                               silu[:, f % 2, :], ALU.mult, ALU.mult).then_inc(empty(f"gu{f}"), 1)

            def result_add(r):
                after(dve, "result_free", r, 1)
                for t in range(TT):
                    job_filled(dve, f"down{t}", r)
                    nc.vector.scalar_tensor_tensor(result[:, t, :], bank(f"down{t}")[:, :], UNDO_HW, h2[:, t, :], ALU.mult,
                                                   ALU.add).then_inc(empty(f"down{t}"), 1)

            att = dict(dft0=lambda s: halves_joined(0, s), dft1=dft, xt=lambda s: lows("xt", xt_lo, xt_hi, "xt_hi", 1.0, s), ba=ba,
                       k=lambda s: taps("k", s), q=lambda s: taps("q", s), v=lambda s: taps("v", s), norm=norm,
                       kk=lambda s: gram("kk", nt, s), qk=lambda s: gram("qk", pt, s), t0=t0, r1=r1, o=o,
                       ot=lambda s: lows("ot", xt_lo, xt_hi, "og_hi", A_UP, s), h=h_add)

            def body(s, r):
                for stage in STAGES:
                    if stage in att and s is not None:
                        att[stage](s)
                    elif stage == "yt" and r is not None:
                        lows("yt", yt_lo, yt_hi, "yt_hi", 1.0, r)
                    elif stage[:3] == "tct" and s is not None:
                        merge(int(stage[-1]), s)
                    elif stage[0] == "u" and r is not None:
                        hidden(int(stage[1:]), r)
                    elif stage == "out" and r is not None:
                        result_add(r)

            run(dve, body)


def build(nc, x, sqrt_eig, pct, w_all, dft, consts, conv, ba, norm, gate, out):
    z = nc.dram_tensor("z_rows", [2 * (ORDERS - 1), SEQS, T], F32, kind="Internal").ap()
    with ExitStack() as ctx:
        banks = [ctx.enter_context(nc.psum_tensor(f"bank{i}", [P, 512], F32)) for i in range(8)]
        w_hi = ctx.enter_context(nc.sbuf_tensor("w_hi", [P, ALL_COLS], F16))
        w_lo = ctx.enter_context(nc.sbuf_tensor("w_lo", [P, ALL_COLS], F16))
        weight_phase(nc, banks, w_all, w_hi, w_lo)
        legendre_phase(nc, banks, x, sqrt_eig, pct, z)
        sequence_phase(nc, banks, z, dft, consts, dict(conv=conv, ba=ba, norm=norm, gate=gate), w_hi, w_lo, out)


def shape_constants():
    n = 2 * NLAT
    j = np.arange(n)
    m = np.arange(NLAT)
    ang = 2 * np.pi * ((m[:, None] * j[None]) % n) / n
    re = np.where(m[:, None] == 0, 1.0, 2.0) * np.cos(ang)
    im = -2.0 * np.sin(ang)
    im[0] = np.cos(np.pi * j)
    dft = np.concatenate([re[0::2], im[0::2], re[1::2], im[1::2]])[:, :NLAT].astype(np.float32)
    i = np.arange(P)
    mats = [np.eye(P), i[:, None] <= i[None], np.ones((P, P)), i[:, None] > i[None]]
    for lv in range(LEVELS):
        b = i >> lv
        mats.append((b[:, None] % 2 == 0) & (b[None] == b[:, None] + 1))
    return dft, np.concatenate([a.astype(np.float32) for a in mats], 1)


def kernel(**inputs):
    import numpy as _np
    import concourse.bacc as _bacc
    from concourse import mybir as _mybir
    from concourse.bass_utils import run_bass_kernel_spmd as _run

    a = {k: _np.asarray(v) for k, v in inputs.items()}
    chunked = lambda w: w.T.reshape(-1, P, w.shape[0]).transpose(1, 0, 2).reshape(P, -1)
    names = ["L0_ffn_w_gate", "L0_ffn_w_up", "L0_ffn_w_down"] + [f"L0_attn_{t}_proj_w" for t in "qkvgo"]
    w_all = _np.concatenate([chunked(a[n]) for n in names], 1)
    conv = _np.stack([a[f"L0_attn_{t}_conv_w"].reshape(DC, P, TAPS).transpose(1, 0, 2) for t in "qkv"], 1)
    ba = _np.stack([a["L0_attn_b_proj_w"][0], a["L0_attn_a_proj_w"][0]], 1).reshape(DC, P, 2).transpose(1, 0, 2)
    norm = _np.broadcast_to(a["L0_attn_o_norm_w"], (P, D))
    gate = _np.broadcast_to(_np.stack([a["L0_attn_A_log"][0], a["L0_attn_dt_bias"][0]]), (P, 2))
    dft, consts = shape_constants()
    arrays = dict(x=a["x"], sqrt_eig=a["L0_tok_sqrt_eig"], pct=a["L0_tok_pct"], w_all=w_all, dft=dft, consts=consts,
                  conv=conv, ba=ba, norm=norm, gate=gate)
    arrays = {f"in_{k}": _np.ascontiguousarray(v) for k, v in arrays.items()}
    nc = _bacc.Bacc("TRN2", target_bir_lowering=False, num_devices=1)
    args = [nc.dram_tensor(k, v.shape, _mybir.dt.from_np(v.dtype), kind="ExternalInput").ap() for k, v in arrays.items()]
    out = nc.dram_tensor("out_0", (SEQS, T, D), F32, kind="ExternalOutput").ap()
    build(nc, *args, out)
    r = _run(nc, [arrays], core_ids=[0])
    return r.results[0]["out_0"]
```

```python
from contextlib import ExitStack

import numpy as np
import concourse.bass as bass
from concourse import mybir

F32 = mybir.dt.float32
F16 = mybir.dt.float16
ALU = mybir.AluOpType
ACT = mybir.ActivationFunctionType
AX = mybir.AxisListType

P = 128
SEQS, NLAT, ORDERS = 32, 256, 257
T = NLAT
TT = T // P
D = 512
DC = D // P
FFN = 1408
FC = FFN // P
TAPS = 4
HP = P // 2
LEVELS = 7

A_UP, W_UP, H_UP = 64.0, 256.0, 16.0
UNDO_AW = 1.0 / (A_UP * W_UP)
UNDO_HW = 1.0 / (H_UP * W_UP)
LN_EPS, L2_EPS, RMS_EPS, Q_EPS = 1e-5, 1e-6, 1e-5, 1e-5

GU_COLS = 2 * DC * FFN
DN_COLS = FC * D
AT_COLS = 5 * DC * D
QUANT_COLS = GU_COLS + DN_COLS
ALL_COLS = QUANT_COLS + AT_COLS
MB = 64
MC = 4


def load_phase(nc, banks, x, sqrt_eig, pct, z, w_all, w_hi, w_lo):
    J = NLAT // P
    BLOCKS = (ORDERS - 1) // MB
    LOOPS = MB // (2 * MC)
    STEPS = BLOCKS * LOOPS
    QW, AW = QUANT_COLS // (2 * STEPS), AT_COLS // (2 * STEPS)
    W_X = 2 * (MB + 1)
    NX = SEQS // LOOPS
    R = 2 * SEQS
    with ExitStack() as ctx:
        sb = lambda n, s, d=F32: ctx.enter_context(nc.sbuf_tensor(n, s, d))
        sem = lambda n: ctx.enter_context(nc.semaphore(n))
        xin = [sb(f"x_in{i}", [P, J, SEQS, W_X if i == (BLOCKS - 1) % 2 else 2 * MB]) for i in range(2)]
        eig = sb("eig", [P, J, ORDERS])
        table = [sb(f"table{i}", [P, MC, J * T]) for i in range(2)]
        xs = [sb(f"x_scaled{i}", [P, J, MC, R]) for i in range(2)]
        stage = sb("z_stage", [2 * R, MC, T])
        RING = 4
        raw = [sb(f"w_raw{i}", [P, QW]) for i in range(RING)]
        plain = [sb(f"w_plain{i}", [P, AW]) for i in range(RING)]
        scale = [sb(f"w_scale{i}", [P, QW]) for i in range(2)]
        above = [sb(f"w_above{i}", [P, QW], F16) for i in range(2)]
        below = [sb(f"w_below{i}", [P, QW], F16) for i in range(2)]
        ones = sb("w_ones", [P, P])
        eig_loaded = sem("eig_loaded")
        x_loaded = [sem(f"x_loaded{i}") for i in range(2)]
        t_loaded = [sem(f"t_loaded{i}") for i in range(2)]
        x_scaled = [sem(f"x_scaled_set{i}") for i in range(2)]
        summed = [sem(f"l_summed{i}") for i in range(2)]
        copied = [sem(f"l_copied{i}") for i in range(2)]
        stored = [sem(f"l_stored{i}") for i in range(2)]
        w_loaded = [sem(f"w_loaded{i}") for i in range(RING)]
        ones_set, mag_set, w_summed, scaled, below_set, tern, quant, delta, final, hi_set, lo_set = (
            sem(f"w_{n}") for n in ("ones_set", "mag_set", "summed", "scaled", "below_set", "tern", "quant", "delta",
                                    "final", "hi_set", "lo_set"))
        block = ctx.enter_context(nc.Block())

        x_v = x.rearrange("n (p j) m c -> j p n (m c)", j=J)
        pct_v = pct.rearrange("m (p j) k -> p m (j k)", j=J)
        z_re = z[0:ORDERS - 1].rearrange("m n k -> n m k")
        z_im = z[ORDERS - 1:2 * (ORDERS - 1)].rearrange("m n k -> n m k")

        def loop(engine, b, body):
            if b == 0:
                body(b, 0, 0)
                body(b, 1, 1)
            with engine.Fori(1 if b == 0 else 0, LOOPS // 2) as v:
                body(b, v * 2, 0)
                body(b, v * 2 + 1, 1)

        def wait_past(engine, semaphore, value):
            if not isinstance(value, int) or value > 0:
                engine.wait_ge(semaphore, value)

        def behind(b, u, q, h, lag):
            step = u + (b * LOOPS - (lag + 1 - h) // 2)
            return None if isinstance(step, int) and step < 0 else (step, (h - lag) % 2, (2 * q + h - lag) % RING)

        count = lambda step, h: step * 2 + (h + 1)
        q_cols = lambda step, h: bass.ds(step * (2 * QW) + h * QW, QW)
        a_cols = lambda step, h: bass.ds(step * (2 * AW) + (h * AW + QUANT_COLS), AW)

        @block.sync
        def _(sp):
            at = lambda v: v if isinstance(v, int) else sp.snap(v)
            sp.dma_start(eig[:, :, :], sqrt_eig.rearrange("a (p j) m -> p (a j) m", j=J)).then_inc(eig_loaded, 16)

            def load_step(b, u, q):
                for h in range(2):
                    m0 = at(u * (2 * MC) + (b * MB + h * MC))
                    q0 = at(u * (2 * QW) + (b * LOOPS * 2 * QW + h * QW))
                    a0 = at(u * (2 * AW) + (b * LOOPS * 2 * AW + h * AW + QUANT_COLS))
                    wait_past(sp, summed[h], u + b * LOOPS)
                    sp.dma_start(table[h][:, :, :], pct_v[:, bass.ds(m0, MC), :]).then_inc(t_loaded[h], 16)
                    wait_past(sp, lo_set, u * 2 + (b * LOOPS * 2 + h + 1 - RING))
                    sp.dma_start(raw[2 * q + h][:, :], w_all[:, bass.ds(q0, QW)]).then_inc(w_loaded[2 * q + h], 16)
                    sp.dma_start(plain[2 * q + h][:, :], w_all[:, bass.ds(a0, AW)]).then_inc(w_loaded[2 * q + h], 16)
                if b + 1 < BLOCKS:
                    w = 2 * (MB + (b + 1 == BLOCKS - 1))
                    n0 = at(u * NX)
                    for j in range(J):
                        sp.dma_start(xin[(b + 1) % 2][:, j, bass.ds(n0, NX), 0:w],
                                     x_v[j, :, bass.ds(n0, NX), 2 * MB * (b + 1):2 * MB * (b + 1) + w])\
                            .then_inc(x_loaded[(b + 1) % 2], 16)

            for n0 in range(0, SEQS, NX):
                for j in range(J):
                    sp.dma_start(xin[0][:, j, n0:n0 + NX, 0:2 * MB], x_v[j, :, n0:n0 + NX, 0:2 * MB]).then_inc(x_loaded[0], 16)
            for b in range(BLOCKS):
                loop(sp, b, load_step)
            sp.wait_ge(summed[0], STEPS)
            sp.dma_start(table[0][:, 0, :], pct_v[:, ORDERS - 1, :]).then_inc(t_loaded[0], 16)

        @block.vector
        def _(dve):
            def scale_x(b, h, m, e, n_orders):
                for j in range(J):
                    xv = xin[b % 2][:, j, :, :].rearrange("p n (m c) -> p m c n", c=2)
                    ins = nc.vector.tensor_tensor(
                        xs[h][:, j, 0:n_orders, :].rearrange("p m (c n) -> p m c n", c=2),
                        xv[:, bass.ds(m, n_orders), :, :],
                        eig[:, j, bass.ds(e, n_orders)].unsqueeze(2).unsqueeze(3).to_broadcast([P, n_orders, 2, SEQS]),
                        ALU.mult)
                ins.then_inc(x_scaled[h], 1)

            def compare(step, h, place):
                r, s = raw[place], scale[h]
                dve.wait_ge(w_summed, count(step, h))
                nc.vector.tensor_scalar(s[:, :], banks[4 + h][:, 0:QW], 1.0 / P, Q_EPS, ALU.mult, ALU.add).then_inc(scaled, 1)
                dve.wait_ge(scaled, count(step, h))
                nc.vector.scalar_tensor_tensor(above[h][:, :], s[:, :], 0.5, r[:, :], ALU.mult, ALU.is_lt)
                nc.vector.scalar_tensor_tensor(below[h][:, :], s[:, :], -0.5, r[:, :], ALU.mult, ALU.is_gt).then_inc(below_set, 1)

            def low(step, h, place):
                dve.wait_ge(hi_set, count(step, h))
                nc.vector.scalar_tensor_tensor(w_lo[:, a_cols(step, h)], plain[place][:, :], W_UP, w_hi[:, a_cols(step, h)],
                                               ALU.mult, ALU.subtract)
                nc.vector.scalar_tensor_tensor(w_lo[:, q_cols(step, h)], raw[place][:, :], W_UP, w_hi[:, q_cols(step, h)],
                                               ALU.mult, ALU.subtract).then_inc(lo_set, 1)

            def vector_step(b, u, q):
                for h in range(2):
                    wait_past(dve, summed[h], u + b * LOOPS)
                    scale_x(b, h, u * (2 * MC) + h * MC, u * (2 * MC) + (b * MB + h * MC), MC)
                    if behind(b, u, q, h, 1):
                        compare(*behind(b, u, q, h, 1))
                    if behind(b, u, q, h, 2):
                        low(*behind(b, u, q, h, 2))

            dve.wait_ge(eig_loaded, 16)
            for b in range(BLOCKS):
                dve.wait_ge(x_loaded[b % 2], 16 * J * LOOPS * (b // 2 + 1))
                loop(dve, b, vector_step)
            compare(STEPS - 1, 1, RING - 1)
            low(STEPS - 1, 0, RING - 2)
            low(STEPS - 1, 1, RING - 1)
            dve.wait_ge(summed[0], STEPS)
            scale_x(BLOCKS - 1, 0, MB, ORDERS - 1, 1)

        @block.tensor
        def _(pe):
            def order(h, i, bank, col):
                for j in range(J):
                    mm = nc.tensor.matmul(bank[R * h:R * h + R, col:col + T], xs[h][:, j, i, :],
                                          table[h][:, i, j * T:(j + 1) * T], start=(j == 0), stop=(j == J - 1))
                return mm

            def tensor_step(b, u, q):
                for h in range(2):
                    pe.wait_ge(x_scaled[h], u + (b * LOOPS + 1))
                    pe.wait_ge(t_loaded[h], u * 16 + (b * LOOPS + 1) * 16)
                    wait_past(pe, copied[h], u + b * LOOPS)
                    for i in range(MC):
                        mm = order(h, i, banks[2 * h + i // 2], (i % 2) * T)
                    mm.then_inc(summed[h], 1)
                    pe.wait_ge(mag_set, u * 2 + (b * LOOPS * 2 + h + 1))
                    wait_past(pe, scaled, u * 2 + (b * LOOPS * 2 + h - 1))
                    nc.tensor.matmul(banks[4 + h][:, 0:QW], ones[:, :], scale[h][:, :], start=True, stop=True).then_inc(w_summed, 1)

            pe.wait_ge(ones_set, 1)
            for b in range(BLOCKS):
                loop(pe, b, tensor_step)
            pe.wait_ge(x_scaled[0], STEPS + 1)
            pe.wait_ge(t_loaded[0], 16 * (STEPS + 1))
            pe.wait_ge(copied[0], STEPS)
            order(0, 0, banks[0], 0).then_inc(summed[0], 1)

        @block.scalar
        def _(act):
            at = lambda v: v if isinstance(v, int) else act.snap(v)

            def high(step, h, place):
                act.wait_ge(final, count(step, h))
                nc.scalar.activation(w_hi[:, a_cols(step, h)], plain[place][:, :], ACT.Copy, scale=W_UP)
                nc.scalar.activation(w_hi[:, q_cols(step, h)], raw[place][:, :], ACT.Copy, scale=W_UP).then_inc(hi_set, 1)

            def scalar_step(b, u, q):
                for h in range(2):
                    m0 = at(u * (2 * MC) + (b * MB + h * MC))
                    act.wait_ge(w_loaded[2 * q + h], u * 16 + (b * LOOPS - q + 2) * 16)
                    nc.scalar.activation(scale[h][:, :], raw[2 * q + h][:, :], ACT.Abs).then_inc(mag_set, 1)
                    act.wait_ge(summed[h], u + (b * LOOPS + 1))
                    wait_past(act, stored[h], u * 32 + b * LOOPS * 32)
                    half = slice(R * h, R * h + R)
                    for k in range(2):
                        ins = nc.scalar.activation(stage[half, 2 * k:2 * k + 2, :].rearrange("p m k -> p (m k)"),
                                                   banks[2 * h + k][half, :], ACT.Copy)
                    ins.then_inc(copied[h], 1)
                    if behind(b, u, q, h, 1):
                        high(*behind(b, u, q, h, 1))
                    act.wait_ge(copied[h], u + (b * LOOPS + 1))
                    act.dma_start(z_re[:, bass.ds(m0, MC), :], stage[R * h:R * h + SEQS, :, :]).then_inc(stored[h], 16)
                    act.dma_start(z_im[:, bass.ds(m0, MC), :], stage[R * h + SEQS:R * h + R, :, :]).then_inc(stored[h], 16)

            for b in range(BLOCKS):
                loop(act, b, scalar_step)
            high(STEPS - 1, 1, RING - 1)
            act.wait_ge(summed[0], STEPS + 1)
            for h in range(2):
                act.wait_ge(stored[h], STEPS * 32)
            nc.scalar.activation(stage[0:R, 0, :], banks[0][0:R, 0:T], ACT.Copy).then_inc(copied[0], 1)
            act.wait_ge(copied[0], STEPS + 1)
            act.dma_start(z[ORDERS - 1], stage[0:SEQS, 0, :]).then_inc(stored[0], 16)
            act.wait_ge(stored[0], STEPS * 32 + 16)

        @block.gpsimd
        def _(pool):
            nc.gpsimd.memset(ones[:, :], 1.0).then_inc(ones_set, 1)

            def quantise(b, u, q):
                for h in range(2):
                    n = u * 2 + (b * LOOPS * 2 + h + 1)
                    r, s, a = raw[2 * q + h], scale[h], above[h]
                    pool.wait_ge(below_set, n)
                    nc.gpsimd.tensor_tensor(a[:, :], a[:, :], below[h][:, :], ALU.subtract).then_inc(tern, 1)
                    pool.wait_ge(tern, n)
                    nc.gpsimd.tensor_tensor(s[:, :], a[:, :], s[:, :], ALU.mult).then_inc(quant, 1)
                    pool.wait_ge(quant, n)
                    nc.gpsimd.tensor_tensor(s[:, :], s[:, :], r[:, :], ALU.subtract).then_inc(delta, 1)
                    pool.wait_ge(delta, n)
                    nc.gpsimd.tensor_tensor(r[:, :], r[:, :], s[:, :], ALU.add).then_inc(final, 1)

            for b in range(BLOCKS):
                loop(pool, b, quantise)


STAGES = """dft0 yt dft1 g0 u0 e0 g1 u1 e1 xt g2 u2 ba k e2 q v g3 u3 d0 g4 norm e3 decay kk qk d1 gate0 t0 u4 ct1
gate1 tct1 e4 d2 ct2 g5 tct2 vt ct3 u5 tct3 e5 d3 ct4 g6 tct4 u6 ct5 e6 d4 tct5 g7 ct6 u7 tct6 e7 d5 w0 g8 r1 u8 w1
d6 e8 o g9 u9 d7 e9 ot g10 u10 e10 h d8 d9 d10 out keep""".split()

STAGE_JOBS = {"xt": ["xt0", "xt1"], "k": ["k0", "k1"], "q": ["q0", "q1"], "v": ["v0", "v1"],
              "vt": ["vt0", "vt1"], "o": ["o0", "o1"], "ot": ["ot0", "ot1"], "h": ["h0", "h1"]}
FFN_STAGES = {f"{kind}{f}" for kind in "gude" for f in range(FC)} | {"yt", "out", "keep"}
ATT_JOBS = [j for st in STAGES if st not in FFN_STAGES for j in STAGE_JOBS.get(st, [st])]
SKIPS = ["k1", "norm", "vt1"][:-len(ATT_JOBS) % 4]
BANK_OF = {j: (n + sum(ATT_JOBS.index(k) < n for k in SKIPS)) % 4 for n, j in enumerate(ATT_JOBS)}
BANK_OF.update({f"yt{i}": 4 + i for i in range(2)})
BANK_OF.update({f"gu{f}": 4 + f % 2 for f in range(FC)})
BANK_OF.update({f"down{t}": 6 + t for t in range(TT)})
PER_BANK = [sum(1 for b in BANK_OF.values() if b == k) for k in range(8)]
ORDINAL = {j: [i for i in BANK_OF if BANK_OF[i] == b].index(j) for j, b in BANK_OF.items()}


def sequence_phase(nc, banks, z, dft, consts, small, w_hi, w_lo, out):
    with ExitStack() as ctx:
        sb = lambda n, s, d=F32: ctx.enter_context(nc.sbuf_tensor(n, s, d))
        sem = lambda n: ctx.enter_context(nc.semaphore(n))
        dft_sb = sb("dft_sb", [P, DC, T])
        cst = sb("cst", [P, (LEVELS + 4) * P])
        ident, triu_ones, triu, low = (cst[:, 0:P], cst[:, P:3 * P], cst[:, P:2 * P], cst[:, 3 * P:4 * P])
        ones = cst[:, 2 * P:3 * P]
        masks = cst[:, 4 * P:].rearrange("p (l i) -> p l i", i=P)
        conv_w = sb("conv_w", [P, 3, DC, TAPS])
        ba_w = sb("ba_w", [P, DC, 2])
        ba_hi, ba_lo = sb("ba_hi", [P, DC, 2], F16), sb("ba_lo", [P, DC, 2], F16)
        norm_w = sb("norm_w", [P, D])
        gate_c = sb("gate_c", [P, 2])
        exps = sb("exps", [P, 2, TT])
        z_in = sb("z_in", [P, DC, T])
        h = sb("h", [P, TT, D])
        xn = sb("xn", [P, TT, D])
        xt_hi, xt_lo = sb("xt_hi", [P, DC, T], F16), sb("xt_lo", [P, DC, T], F16)
        ch = {t: sb(f"ch_{t}", [P, DC, T]) for t in "kqv"}
        v_tok = sb("v_tok", [P, TT, D])
        gate = sb("gate", [P, TT, D])
        decay = sb("decay", [P, 4 * P])
        odd = decay[:, :].rearrange("p (t j) -> p t j", t=TT)
        nt, pt = sb("nt", [P, 4 * P]), sb("pt", [P, 4 * P])
        gm = sb("gm", [P, 3, P])
        ct = sb("ct", [P, LEVELS, TT, P])
        inv = sb("inv", [P, 2, TT, P])
        c_t = sb("c_t", [P, LEVELS - 1, TT, P])
        w_tok = sb("w_tok", [P, TT, D])
        rhs1 = sb("rhs1", [P, D])
        h2 = sb("h2", [P, TT, D])
        yt_hi, yt_lo = sb("yt_hi", [P, DC, T], F16), sb("yt_lo", [P, DC, T], F16)
        RING = 4
        silu = sb("silu", [P, 2, T])
        hid = sb("hid", [P, 2, T])
        hid_hi, hid_lo = sb("hid_hi", [P, RING, T], F16), sb("hid_lo", [P, RING, T], F16)
        result = sb("result", [P, TT, D])
        stats = [sb(f"stats{i}", [P, TT, 6]) for i in range(2)]
        moments = [sb(f"moments{i}", [P, TT, 3]) for i in range(2)]
        mean, gap_sq, m2 = ([sb(f"{n}{i}", [P, TT]) for i in range(2)] for n in ("mean", "gap_sq", "m2"))
        var_e = [sb(f"var_e{i}", [P, TT]) for i in range(2)]
        rstd = [sb(f"rstd{i}", [P, TT]) for i in range(2)]
        zba = sb("zba", [P, TT])
        earg = sb("earg", [P, 2, TT])
        eval_ = sb("eval", [P, 2, TT])
        ln1p = sb("ln1p", [P, TT])
        beta1, beta = sb("beta1", [P, TT]), sb("beta", [P, TT])
        gpos, g = sb("gpos", [P, TT]), sb("g", [P, TT])
        ss = sb("ss", [P, 2, TT])
        rss, c_col, n_col = sb("rss", [P, TT]), sb("c_col", [P, TT]), sb("n_col", [P, TT])
        q_eps, o_ss, o_arg, o_scale = (sb(n, [P, TT]) for n in ("q_eps", "o_ss", "o_arg", "o_scale"))
        o_sq = rhs1

        gu = lambda w, which: w[:, 0:GU_COLS].rearrange("p (t c f) -> p t c f", t=2, c=DC)[:, which]
        dn = lambda w: w[:, GU_COLS:QUANT_COLS].rearrange("p (c o) -> p c o", c=FC)
        at = lambda w, which: w[:, QUANT_COLS:].rearrange("p (t c o) -> p t c o", t=5, c=DC)[:, "qkvgo".index(which)]

        filled = [sem(f"bank_filled{b}") for b in range(8)]
        emptied = [sem(f"bank_emptied{b}") for b in range(8)]
        PER = dict(z_loaded=32, odd=TT, result_free=32, stats=TT, moments=2, mean=1, gap_sq=1, m2=1, var_e=1, rstd=1, xn=TT, xt_hi=2,
                   ba_a=1, ba_exp=1, ba_ln=1, beta1=1, beta=1, gpos=1, g=1, gm=3,
                   tap1=12, taps=30, silu_k=1, silu_q=1, silu_v=1, sq_k=1, sq_q=1, sq_half=2, sq_sum=2, gate_w=1, kept=1,
                   rss=1, c_col=1, n_col=1, q_eps=1, decay_set=1, ct=LEVELS, s0=1,
                   o_ss=2, o_arg=1, o_scale=1, og_hi=2,
                   stats2=TT, moments2=2, mean2=1, gap_sq2=1, m22=1, var_e2=1, rstd2=1, yn=TT, yt_hi=2,
                   silu=FC, hid_hi=FC, hid_lo=FC)
        sems = {n: sem(n) for n in PER}

        def level_cols(ap, lv, odd_blocks):
            if len(ap.shape) == 2:
                return ap.rearrange("p (b e i) -> p e b i", e=2, i=1 << lv)[:, odd_blocks]
            return ap.rearrange("p t (b e i) -> p e t b i", e=2, i=1 << lv)[:, odd_blocks]

        def after(eng, step, s, k=None):
            v = s * PER[step] + (PER[step] if k is None else k)
            if not isinstance(v, int) or v > 0:
                eng.wait_ge(sems[step], v)

        def job_filled(eng, job, s):
            b = BANK_OF[job]
            eng.wait_ge(filled[b], s * PER_BANK[b] + ORDINAL[job] + 1)

        def job_emptied(eng, job, s):
            b = BANK_OF[job]
            eng.wait_ge(emptied[b], s * PER_BANK[b] + ORDINAL[job] + 1)

        def bank_free(eng, job, s):
            b = BANK_OF[job]
            v = s * PER_BANK[b] + ORDINAL[job]
            if not isinstance(v, int) or v > 0:
                eng.wait_ge(emptied[b], v)

        def bank(job):
            return banks[BANK_OF[job]]

        def earlier(s):
            return not isinstance(s, int) or s > 0

        const_loaded, setup_act, setup_dve = sem("const_loaded"), sem("setup_act"), sem("setup_dve")
        setup_pool = sem("setup_pool")
        z_v = z.rearrange("(w r e) n k -> n e r w k", w=2, e=2)

        def run(engine, body):
            body(0, None)
            with engine.Fori(1, SEQS) as s:
                body(s, s - 1)
            body(None, SEQS - 1)

        block = ctx.enter_context(nc.Block())

        @block.sync
        def _(sp):
            for dst, src in ((dft_sb, dft.rearrange("(c r) j -> r c j", c=DC)), (cst, consts), (conv_w, small["conv"]),
                             (ba_w, small["ba"]), (norm_w, small["norm"]), (gate_c, small["gate"])):
                sp.dma_start(dst[:], src).then_inc(const_loaded, 16)
            def load_z(n):
                for e in range(2):
                    sp.dma_start(z_in[:, 2 * e:2 * e + 2, :], z_v[n, e]).then_inc(sems["z_loaded"], 16)

            load_z(0)

            def body(s, r):
                if s is not None and not (isinstance(s, int) and s == SEQS - 1):
                    nxt = s + 1 if isinstance(s, int) else sp.snap(s + 1)
                    job_filled(sp, "dft1", s)
                    load_z(nxt)
                if r is not None:
                    rr = r if isinstance(r, int) else sp.snap(r)
                    for t in range(TT):
                        job_emptied(sp, f"down{t}", r)
                        sp.dma_start(out[rr, t * P:(t + 1) * P, :], result[:, t, :]).then_inc(sems["result_free"], 16)

            body(0, None)
            with sp.Fori(1, SEQS - 1) as s:
                body(s, s - 1)
            body(SEQS - 1, SEQS - 2)
            body(None, SEQS - 1)
            after(sp, "result_free", SEQS - 1, 33)

        @block.tensor
        def _(pe):
            pe.wait_ge(const_loaded, 6 * 16)
            pe.wait_ge(setup_dve, 3)

            def pairs(out_ap, lhs, rhs, cols_l, cols_r, chunks, opened=True, closed=True, second_half=None):
                n = 0
                for c in range(chunks):
                    if c == 2 and second_half:
                        second_half()
                    for a, b in ((0, 0), (0, 1), (1, 0)):
                        mm = nc.tensor.matmul(out_ap, lhs[a][:, c, cols_l], rhs[b][:, c, cols_r],
                                              start=opened and n == 0, stop=closed and n == 3 * chunks - 1)
                        n += 1
                return mm

            XT, YT = (xt_hi, xt_lo), (yt_hi, yt_lo)
            sl = lambda a, n: slice(a, a + n)

            def full(job):
                return filled[BANK_OF[job]]

            def dft(t, s):
                after(pe, "z_loaded", s)
                bank_free(pe, f"dft{t}", s)
                for e in range(2):
                    for c in range(2 * e, 2 * e + 2):
                        mm = nc.tensor.matmul(bank(f"dft{t}")[:, sl(e * T, T)], z_in[:, c, sl(t * P, P)],
                                              dft_sb[:, c, :], start=(c == 2 * e), stop=(c == 2 * e + 1))
                mm.then_inc(full(f"dft{t}"), 1)

            def transposes(kind, src, s):
                for half in range(2):
                    job = f"{kind}{half}"
                    if kind != "yt":
                        bank_free(pe, job, s)
                    for cc in range(2):
                        for t in range(TT):
                            mm = nc.tensor.transpose(bank(job)[:, sl(cc * T + t * P, P)],
                                                     src[:, t, sl((2 * half + cc) * P, P)], ident)
                    mm.then_inc(full(job), 1)

            def xt(s):
                after(pe, "xn", s)
                transposes("xt", xn, s)

            def ba(s):
                job_emptied(pe, "xt0", s)
                bank_free(pe, "ba", s)
                for t in range(TT):
                    mm = pairs(bank("ba")[:, sl(2 * t, 2)], XT, (ba_hi, ba_lo), sl(t * P, P), slice(None), DC,
                               second_half=None if t else lambda: job_emptied(pe, "xt1", s))
                mm.then_inc(full("ba"), 1)

            def channels(which, s):
                w = (at(w_hi, which), at(w_lo, which))
                for i in range(2):
                    job = f"{which}{i}"
                    bank_free(pe, job, s)
                    for oc in range(2):
                        mm = pairs(bank(job)[:, sl(oc * T, T)], w, XT, sl((2 * i + oc) * P, P), slice(None), DC)
                    mm.then_inc(full(job), 1)

            def gate_job(t, s):
                job = f"gate{t}"
                bank_free(pe, job, s)
                w = (at(w_hi, "g"), at(w_lo, "g"))
                pairs(bank(job)[:, :], XT, w, sl(t * P, P), slice(None), DC).then_inc(full(job), 1)

            def norm(s):
                after(pe, "sq_sum", s)
                bank_free(pe, "norm", s)
                for n, buf in enumerate((xn, w_tok)):
                    for t in range(TT):
                        mm = nc.tensor.matmul(bank("norm")[:, 2 * n + t:2 * n + t + 1], buf[:, 0, sl(t * P, P)],
                                              ones[:, 0:1], start=True, stop=True)
                mm.then_inc(full("norm"), 1)

            def decay_job(s):
                after(pe, "gm", s)
                bank_free(pe, "decay", s)
                b = bank("decay")
                nc.tensor.matmul(b[:, 0:2 * P], gm[:, 0, :], triu_ones, start=True, stop=False)
                nc.tensor.matmul(b[:, P:2 * P], gm[:, 2, :], triu, start=False, stop=True)
                nc.tensor.matmul(b[:, 2 * P:3 * P], gm[:, 1, :], triu, start=True, stop=True).then_inc(full("decay"), 1)

            def gram(job, which, s):
                after(pe, "silu_k", s)
                after(pe, f"silu_{which}", s)
                bank_free(pe, job, s)
                for cols, j0, n in ((0, 0, 2 * P), (2 * P, P, P)):
                    for c in range(DC):
                        mm = nc.tensor.matmul(bank(job)[:, sl(cols, n)], ch["k"][:, c, sl(j0, P)],
                                              ch[which][:, c, sl(j0, n)], start=(c == 0), stop=(c == DC - 1))
                mm.then_inc(full(job), 1)

            def t0(s):
                after(pe, "s0", s)
                bank_free(pe, "t0", s)
                for t in range(TT):
                    mm = nc.tensor.transpose(bank("t0")[:, sl(t * P, P)], inv[:, 1, t, :], ident)
                mm.then_inc(full("t0"), 1)

            def vt(s):
                after(pe, "silu_v", s)
                for t in range(TT):
                    job = f"vt{t}"
                    bank_free(pe, job, s)
                    for c in range(DC):
                        mm = nc.tensor.transpose(bank(job)[:, sl(c * P, P)], ch["v"][:, c, sl(t * P, P)], ident)
                    mm.then_inc(full(job), 1)

            def ct_job(lv, s):
                job_emptied(pe, "t0" if lv == 1 else f"tct{lv - 1}", s)
                after(pe, "ct", s)
                bank_free(pe, f"ct{lv}", s)
                for t in range(TT):
                    mm = nc.tensor.matmul(bank(f"ct{lv}")[:, sl(t * HP, HP)], ct[:, lv, t, :],
                                          level_cols(inv[:, 0, t, :], lv, 0), start=True, stop=True)
                mm.then_inc(full(f"ct{lv}"), 1)

            def tct_job(lv, s):
                job_emptied(pe, f"ct{lv}", s)
                bank_free(pe, f"tct{lv}", s)
                b = bank(f"tct{lv}")
                for t in range(TT):
                    if lv < LEVELS - 1:
                        nc.tensor.matmul(b[:, sl(t * HP, HP)], inv[:, 1, t, :], level_cols(c_t[:, lv - 1, t, :], lv, 0),
                                         start=True, stop=True)
                    mm = nc.tensor.matmul(b[:, sl((2 + t) * HP, HP)], c_t[:, lv - 1, t, :],
                                          level_cols(inv[:, 1, t, :], lv, 1), start=True, stop=True)
                mm.then_inc(full(f"tct{lv}"), 1)

            def w0(s):
                job_emptied(pe, f"tct{LEVELS - 1}", s)
                job_emptied(pe, "vt0", s)
                bank_free(pe, "w0", s)
                nc.tensor.matmul(bank("w0")[:, :], inv[:, 1, 0, :], v_tok[:, 0, :], start=True, stop=True).then_inc(full("w0"), 1)

            def r1(s):
                job_emptied(pe, "w0", s)
                bank_free(pe, "r1", s)
                nc.tensor.matmul(bank("r1")[:, :], nt[:, P:2 * P], w_tok[:, 0, :], start=True, stop=True).then_inc(full("r1"), 1)

            def w1(s):
                job_emptied(pe, "r1", s)
                bank_free(pe, "w1", s)
                nc.tensor.matmul(bank("w1")[:, :], inv[:, 1, 1, :], rhs1[:, :], start=True, stop=True).then_inc(full("w1"), 1)

            def o(s):
                job_emptied(pe, "qk", s)
                bank_free(pe, "o0", s)
                nc.tensor.matmul(bank("o0")[:, :], pt[:, 0:P], w_tok[:, 0, :], start=True, stop=True).then_inc(full("o0"), 1)
                job_emptied(pe, "w1", s)
                bank_free(pe, "o1", s)
                nc.tensor.matmul(bank("o1")[:, :], pt[:, P:2 * P], w_tok[:, 0, :], start=True, stop=False)
                nc.tensor.matmul(bank("o1")[:, :], pt[:, 2 * P:3 * P], w_tok[:, 1, :], start=False, stop=True).then_inc(full("o1"), 1)

            def ot(s):
                job_emptied(pe, "o1", s)
                transposes("ot", v_tok, s)

            def h_job(s):
                job_emptied(pe, "ot0", s)
                w = (at(w_hi, "o"), at(w_lo, "o"))
                for t in range(TT):
                    job = f"h{t}"
                    bank_free(pe, job, s)
                    pairs(bank(job)[:, :], XT, w, sl(t * P, P), slice(None), DC,
                          second_half=None if t else lambda: job_emptied(pe, "ot1", s)).then_inc(full(job), 1)

            def yt(r):
                after(pe, "yn", r)
                transposes("yt", xn, r)

            def g_half(f, r):
                if f == 0:
                    job_emptied(pe, "yt0", r)
                bank_free(pe, f"gu{f}", r)
                pairs(bank(f"gu{f}")[:, 0:T], (gu(w_hi, 0), gu(w_lo, 0)), YT, sl(f * P, P), slice(None), DC,
                      second_half=None if f else lambda: job_emptied(pe, "yt1", r))

            def u_half(f, r):
                pairs(bank(f"gu{f}")[:, T:2 * T], (gu(w_hi, 1), gu(w_lo, 1)), YT, sl(f * P, P), slice(None), DC)\
                    .then_inc(full(f"gu{f}"), 1)

            def d(f, r):
                after(pe, "hid_lo", r, f + 1)
                for t in range(TT):
                    job = f"down{t}"
                    for n, (a, b) in enumerate(((hid_hi, w_hi), (hid_hi, w_lo), (hid_lo, w_hi))):
                        mm = nc.tensor.matmul(bank(job)[:, :], a[:, f % RING, sl(t * P, P)], dn(b)[:, f, :],
                                              start=(f == 0 and n == 0), stop=(f == FC - 1 and n == 2))
                    if f == FC - 1:
                        mm.then_inc(full(job), 1)

            att = dict(dft0=lambda s: dft(0, s), dft1=lambda s: dft(1, s), xt=xt, ba=ba, k=lambda s: channels("k", s), q=lambda s: channels("q", s),
                       v=lambda s: channels("v", s), norm=norm, decay=decay_job, kk=lambda s: gram("kk", "k", s),
                       qk=lambda s: gram("qk", "q", s), gate0=lambda s: gate_job(0, s), gate1=lambda s: gate_job(1, s),
                       t0=t0, vt=vt, w0=w0, r1=r1, w1=w1, o=o, ot=ot, h=h_job)

            def body(s, r):
                for stage in STAGES:
                    if stage in att:
                        if s is not None:
                            att[stage](s)
                    elif stage[:2] == "ct" or stage[:3] == "tct":
                        if s is not None:
                            (ct_job if stage[0] == "c" else tct_job)(int(stage[-1]), s)
                    elif stage == "yt" and r is not None:
                        yt(r)
                    elif r is not None and stage not in ("out", "keep", "yt"):
                        {"g": g_half, "u": u_half, "d": d, "e": lambda f, r: None}[stage[0]](int(stage[1:]), r)

            run(pe, body)

        @block.scalar
        def _(act):
            act.wait_ge(const_loaded, 6 * 16)
            nc.scalar.activation(gate_c[:, 0:1], gate_c[:, 0:1], ACT.Exp).then_inc(setup_act, 1)
            nc.scalar.activation(ba_hi[:, :, :], ba_w[:, :, :], ACT.Copy, scale=W_UP).then_inc(setup_act, 1)
            act.wait_ge(setup_dve, 3)

            def empty(job):
                return emptied[BANK_OF[job]]

            def dft(t, s):
                if earlier(s):
                    job_emptied(act, "h1", s - 1)
                job_filled(act, f"dft{t}", s)
                nc.scalar.activation(odd[:, t, :], bank(f"dft{t}")[:, T:2 * T], ACT.Copy).then_inc(sems["odd"], 1)

            def halves(kind, dst, step, up, s):
                for i in range(2):
                    job_filled(act, f"{kind}{i}", s)
                    nc.scalar.activation(dst[:, 2 * i:2 * i + 2, :].rearrange("p c x -> p (c x)"),
                                         bank(f"{kind}{i}")[:, :], ACT.Copy, scale=up).then_inc(sems[step], 1)

            def xt(s):
                if earlier(s):
                    job_filled(act, "h1", s - 1)
                halves("xt", xt_hi, "xt_hi", 1.0, s)

            def ba(s):
                after(act, "ba_a", s)
                nc.scalar.activation(eval_[:, :, :], earg[:, :, :], ACT.Exp).then_inc(sems["ba_exp"], 1)
                after(act, "ba_exp", s)
                nc.scalar.activation(ln1p[:, :], eval_[:, 1, :], ACT.Ln, bias=1.0).then_inc(sems["ba_ln"], 1)

            def taps(which, s):
                for i in range(2):
                    job_filled(act, f"{which}{i}", s)
                    for oc in range(2):
                        c = 2 * i + oc
                        nc.scalar.activation(ch[which][:, c, :], bank(f"{which}{i}")[:, oc * T:(oc + 1) * T], ACT.Copy,
                                             scale=conv_w[:, "qkv".index(which), c, TAPS - 1:TAPS]).then_inc(sems["tap1"], 1)

            def swish(which, s):
                job_emptied(act, f"{which}1", s)
                flat = ch[which][:, :, :].rearrange("p c x -> p (c x)")
                nc.scalar.activation(flat, flat, ACT.Silu).then_inc(sems[f"silu_{which}"], 1)

            def square(which, buf, s):
                after(act, f"silu_{which}", s)
                nc.scalar.activation(buf[:, :, :].rearrange("p t x -> p (t x)"),
                                     ch[which][:, :, :].rearrange("p c x -> p (c x)"),
                                     ACT.Square).then_inc(sems[f"sq_{which}"], 1)

            def q(s):
                taps("q", s)
                swish("k", s)
                square("k", w_tok, s)

            def v(s):
                taps("v", s)
                swish("q", s)
                square("q", xn, s)

            def decay_exp(s):
                job_filled(act, "decay", s)
                nc.scalar.activation(decay[:, 0:3 * P], bank("decay")[:, 0:3 * P], ACT.Exp).then_inc(empty("decay"), 1)

            def gate_half(t, s):
                job_filled(act, f"gate{t}", s)
                nc.scalar.activation(gate[:, t, :], bank(f"gate{t}")[:, :], ACT.Silu, scale=UNDO_AW).then_inc(empty(f"gate{t}"), 1)

            def t0(s):
                job_filled(act, "t0", s)
                nc.scalar.activation(inv[:, 0, :, :].rearrange("p t x -> p (t x)"), bank("t0")[:, 0:TT * P],
                                     ACT.Copy).then_inc(empty("t0"), 1)

            def vt(s):
                after(act, "n_col", s)
                for t in range(TT):
                    job_filled(act, f"vt{t}", s)
                    nc.scalar.activation(v_tok[:, t, :], bank(f"vt{t}")[:, :], ACT.Copy,
                                         scale=n_col[:, t:t + 1]).then_inc(empty(f"vt{t}"), 1)

            def ct_copy(lv, s):
                job_filled(act, f"ct{lv}", s)
                nc.scalar.activation(level_cols(c_t[:, lv - 1, :, :], lv, 0),
                                     bank(f"ct{lv}")[:, 0:P].rearrange("p (t b i) -> p t b i", t=TT, i=1 << lv),
                                     ACT.Copy).then_inc(empty(f"ct{lv}"), 1)

            def w_copy(t, s):
                job_filled(act, f"w{t}", s)
                nc.scalar.activation(w_tok[:, t, :], bank(f"w{t}")[:, :], ACT.Copy).then_inc(empty(f"w{t}"), 1)

            def o(s):
                for t in range(TT):
                    job_filled(act, f"o{t}", s)
                    if t:
                        after(act, "o_ss", s, t)
                    nc.scalar.activation(o_sq[:, :], bank(f"o{t}")[:, :], ACT.Square,
                                         accum_out=o_ss[:, t:t + 1]).then_inc(sems["o_ss"], 1)

            def silu_f(f, r):
                job_filled(act, f"gu{f}", r)
                nc.scalar.activation(silu[:, f % 2, :], bank(f"gu{f}")[:, 0:T], ACT.Silu, scale=UNDO_AW).then_inc(sems["silu"], 1)

            def hid_high(f, r):
                job_emptied(act, f"gu{f}", r)
                nc.scalar.activation(hid_hi[:, f % RING, :], hid[:, f % 2, :], ACT.Copy).then_inc(sems["hid_hi"], 1)

            def keep(s, r):
                job_emptied(act, "h1", s)
                if r is not None:
                    job_emptied(act, "down1", r)
                nc.scalar.activation(h2[:, :, :], h[:, :, :], ACT.Copy).then_inc(sems["kept"], 1)

            att = dict(dft0=lambda s: dft(0, s), dft1=lambda s: dft(1, s), xt=xt, ba=ba, k=lambda s: taps("k", s), q=q, v=v, norm=lambda s: swish("v", s),
                       decay=decay_exp, gate0=lambda s: gate_half(0, s), gate1=lambda s: gate_half(1, s), t0=t0, vt=vt,
                       w0=lambda s: w_copy(0, s), w1=lambda s: w_copy(1, s), o=o,
                       ot=lambda s: halves("ot", xt_hi, "og_hi", A_UP, s))

            def body(s, r):
                for stage in STAGES:
                    if stage in att and s is not None:
                        att[stage](s)
                    elif stage == "keep" and s is not None:
                        keep(s, r)
                    elif stage == "yt" and r is not None:
                        halves("yt", yt_hi, "yt_hi", 1.0, r)
                    elif stage[:2] == "ct" and s is not None:
                        ct_copy(int(stage[-1]), s)
                    elif stage[0] == "u" and r is not None:
                        silu_f(int(stage[1:]), r)
                    elif stage[0] == "e" and r is not None:
                        hid_high(int(stage[1:]), r)

            run(act, body)

        @block.gpsimd
        def _(pool):
            nc.gpsimd.memset(c_t[:, :, :, :], 0.0).then_inc(setup_pool, 1)
            nc.gpsimd.memset(exps[:, 0, :], -0.5).then_inc(setup_pool, 1)
            nc.gpsimd.memset(exps[:, 1, :], 0.5).then_inc(setup_pool, 1)
            pool.wait_ge(setup_pool, 3)
            pool.wait_ge(const_loaded, 6 * 16)

            def power(dst, src, which, step_in, step_out, s):
                if step_in in BANK_OF:
                    job_emptied(pool, step_in, s)
                else:
                    after(pool, step_in, s)
                nc.gpsimd.tensor_tensor(dst, src, exps[:, which, :], ALU.pow).then_inc(sems[step_out], 1)

            diag = lambda buf: buf[:, :].rearrange("p (t x) -> p t x", t=TT)[:, :, 0:P]

            def square_sums(n, buf, step, s):
                after(pool, step, s)
                nc.gpsimd.tensor_tensor(buf[:, 0, :], buf[:, 0, :], buf[:, 1, :], ALU.add).then_inc(sems["sq_half"], 1)
                after(pool, "sq_half", s, n + 1)
                nc.gpsimd.tensor_tensor(buf[:, 0, 0:T], buf[:, 0, 0:T], buf[:, 0, T:2 * T], ALU.add).then_inc(sems["sq_sum"], 1)

            def decay_mask(s):
                job_emptied(pool, "decay", s)
                nc.gpsimd.tensor_tensor(diag(decay), diag(decay), triu.unsqueeze(1).to_broadcast([P, TT, P]),
                                        ALU.mult).then_inc(sems["decay_set"], 1)

            def level_blocks(s):
                job_emptied(pool, "kk", s)
                for lv in range(LEVELS):
                    nc.gpsimd.tensor_tensor(ct[:, lv, :, :], diag(nt), masks[:, lv, :].unsqueeze(1).to_broadcast([P, TT, P]),
                                            ALU.mult).then_inc(sems["ct"], 1)

            def gate_norm(s):
                job_emptied(pool, "gate0", s)
                job_emptied(pool, "gate1", s)
                nc.gpsimd.tensor_tensor(gate[:, :, :], gate[:, :, :], norm_w[:, :].unsqueeze(1).to_broadcast([P, TT, D]),
                                        ALU.mult).then_inc(sems["gate_w"], 1)

            def hid_low(f, r):
                after(pool, "hid_hi", r, f + 1)
                nc.gpsimd.tensor_tensor(hid_lo[:, f % RING, :], hid[:, f % 2, :], hid_hi[:, f % RING, :],
                                        ALU.subtract).then_inc(sems["hid_lo"], 1)

            att = dict(dft1=lambda s: power(rstd[0][:, :], var_e[0][:, :], 0, "var_e", "rstd", s),
                       q=lambda s: square_sums(0, w_tok, "sq_k", s), v=lambda s: square_sums(1, xn, "sq_q", s),
                       norm=lambda s: power(n_col[:, :], ss[:, 1, :], 1, "norm", "n_col", s),
                       decay=decay_mask, kk=level_blocks, gate1=gate_norm,
                       o=lambda s: power(o_scale[:, :], o_arg[:, :], 0, "o_arg", "o_scale", s),
                       h=lambda s: power(rstd[1][:, :], var_e[1][:, :], 0, "var_e2", "rstd2", s))

            def body(s, r):
                for stage in STAGES:
                    if stage in att and s is not None:
                        att[stage](s)
                    elif stage[0] == "e" and r is not None:
                        hid_low(int(stage[1:]), r)

            run(pool, body)

        @block.vector
        def _(dve):
            dve.wait_ge(const_loaded, 6 * 16)
            dve.wait_ge(setup_act, 2)
            nc.vector.tensor_scalar(gate_c[:, 0:1], gate_c[:, 0:1], -1.0, None, ALU.mult).then_inc(setup_dve, 1)
            nc.vector.tensor_scalar(conv_w[:, :, :, :].rearrange("p a b c -> p (a b c)"),
                                    conv_w[:, :, :, :].rearrange("p a b c -> p (a b c)"), UNDO_AW, None,
                                    ALU.mult).then_inc(setup_dve, 1)
            nc.vector.scalar_tensor_tensor(ba_lo[:, :, :], ba_w[:, :, :], W_UP, ba_hi[:, :, :], ALU.mult,
                                           ALU.subtract).then_inc(setup_dve, 1)
            dve.wait_ge(setup_dve, 3)
            nc.vector.memset(result[:, :, 0:2], 0.0).then_inc(sems["result_free"], 1)

            def empty(job):
                return emptied[BANK_OF[job]]

            def layer_norm(src, src_ready, k, names, dst_free, s):
                n_stats, n_mom, n_mean, n_sq, n_m2, n_var, n_rstd, n_out = names
                for t in range(TT):
                    src_ready(t)
                    nc.vector.bn_stats(stats[k][:, t, :], src[:, t, :]).then_inc(sems[n_stats], 1)
                after(dve, n_stats, s)
                nc.vector.tensor_tensor(moments[k][:, :, 0:2], stats[k][:, :, 1:3], stats[k][:, :, 4:6],
                                        ALU.add).then_inc(sems[n_mom], 1)
                nc.vector.tensor_tensor(moments[k][:, :, 2], stats[k][:, :, 1], stats[k][:, :, 4],
                                        ALU.subtract).then_inc(sems[n_mom], 1)
                after(dve, n_mom, s)
                nc.vector.tensor_scalar(mean[k][:, :], moments[k][:, :, 0], 0.5, None, ALU.mult).then_inc(sems[n_mean], 1)
                nc.vector.scalar_tensor_tensor(gap_sq[k][:, :], moments[k][:, :, 2], D / 4.0, moments[k][:, :, 2], ALU.mult,
                                               ALU.mult).then_inc(sems[n_sq], 1)
                after(dve, n_sq, s)
                nc.vector.tensor_tensor(m2[k][:, :], gap_sq[k][:, :], moments[k][:, :, 1], ALU.add).then_inc(sems[n_m2], 1)
                after(dve, n_m2, s)
                nc.vector.tensor_scalar(var_e[k][:, :], m2[k][:, :], 1.0 / (D * A_UP ** 2), LN_EPS / A_UP ** 2, ALU.mult,
                                        ALU.add).then_inc(sems[n_var], 1)
                dst_free()
                after(dve, n_rstd, s)
                for t in range(TT):
                    nc.vector.tensor_scalar(xn[:, t, :], src[:, t, :], mean[k][:, t:t + 1], rstd[k][:, t:t + 1],
                                            ALU.subtract, ALU.mult).then_inc(sems[n_out], 1)

            def halves_joined(t, s):
                if earlier(s):
                    after(dve, "kept", s - 1)
                    after(dve, "yn", s - 1)
                after(dve, "odd", s, t + 1)
                job_filled(dve, f"dft{t}", s)
                even = bank(f"dft{t}")[:, 0:T]
                nc.vector.tensor_tensor(h[:, t, 0:T], even, odd[:, t, :], ALU.add)
                nc.vector.tensor_tensor(h[:, t, T:2 * T], even, odd[:, t, :], ALU.subtract).then_inc(empty(f"dft{t}"), 1)

            def dft(s):
                halves_joined(1, s)
                layer_norm(h, lambda t: job_emptied(dve, f"dft{t}", s), 0, ("stats", "moments", "mean", "gap_sq", "m2", "var_e", "rstd", "xn"),
                           lambda: earlier(s) and job_filled(dve, "yt1", s - 1), s)

            def lows(kind, dst, hi, step, up, s):
                for i in range(2):
                    after(dve, step, s, i + 1)
                    job_filled(dve, f"{kind}{i}", s)
                    view = lambda b: b[:, 2 * i:2 * i + 2, :].rearrange("p c x -> p (c x)")
                    nc.vector.scalar_tensor_tensor(view(dst), bank(f"{kind}{i}")[:, :], up, view(hi), ALU.mult,
                                                   ALU.subtract).then_inc(empty(f"{kind}{i}"), 1)

            def ba(s):
                job_filled(dve, "ba", s)
                zb = bank("ba")[:, 0:2 * TT].rearrange("p (t w) -> p w t", w=2)
                nc.vector.tensor_scalar(earg[:, 0, :], zb[:, 0, :], -UNDO_AW, None, ALU.mult)
                nc.vector.tensor_scalar(zba[:, :], zb[:, 1, :], UNDO_AW, gate_c[:, 1:2], ALU.mult,
                                        ALU.add).then_inc(empty("ba"), 1)
                job_emptied(dve, "ba", s)
                nc.vector.scalar_tensor_tensor(earg[:, 1, :], zba[:, :], -1.0, zba[:, :], ALU.mult,
                                               ALU.min).then_inc(sems["ba_a"], 1)
                after(dve, "ba_ln", s)
                nc.vector.tensor_scalar(beta1[:, :], eval_[:, 0, :], 1.0, None, ALU.add).then_inc(sems["beta1"], 1)
                nc.vector.scalar_tensor_tensor(gpos[:, :], zba[:, :], 0.0, ln1p[:, :], ALU.max,
                                               ALU.add).then_inc(sems["gpos"], 1)
                after(dve, "beta1", s)
                nc.vector.reciprocal(beta[:, :], beta1[:, :]).then_inc(sems["beta"], 1)
                after(dve, "gpos", s)
                nc.vector.tensor_scalar(g[:, :], gpos[:, :], gate_c[:, 0:1], None, ALU.mult).then_inc(sems["g"], 1)
                after(dve, "g", s)
                for n, (m, t) in enumerate(((low, 0), (low, 1), (ones, 1))):
                    nc.vector.tensor_scalar(gm[:, n, :], m, g[:, t:t + 1], None, ALU.mult).then_inc(sems["gm"], 1)

            def taps(which, s):
                base = "kqv".index(which)
                for i in range(2):
                    job = f"{which}{i}"
                    for tap in range(1, TAPS):
                        for oc in range(2):
                            c = 2 * i + oc
                            if tap == 1 and oc == 0:
                                after(dve, "tap1", s, 4 * base + 2 * i + 2)
                                job_filled(dve, job, s)
                            elif tap > 1:
                                after(dve, "taps", s, 10 * base + 5 * i + 2 * (tap - 2) + oc + 1)
                            dst = ch[which][:, c, tap:T]
                            ins = nc.vector.scalar_tensor_tensor(
                                dst, bank(job)[:, oc * T:(oc + 1) * T - tap],
                                conv_w[:, "qkv".index(which), c, TAPS - 1 - tap:TAPS - tap], dst, ALU.mult, ALU.add)
                            if tap < TAPS - 1 or oc == 0:
                                ins.then_inc(sems["taps"], 1)
                            else:
                                ins.then_inc(empty(job), 1)

            def norm(s):
                job_filled(dve, "norm", s)
                nc.vector.tensor_scalar(ss[:, :, :].rearrange("p w t -> p (w t)"), bank("norm")[:, 0:2 * TT], L2_EPS, None,
                                        ALU.add).then_inc(empty("norm"), 1)
                job_emptied(dve, "norm", s)
                nc.vector.reciprocal(rss[:, :], ss[:, 1, :]).then_inc(sems["rss"], 1)
                nc.vector.tensor_scalar(q_eps[:, :], ss[:, 0, :], RMS_EPS * D, None, ALU.mult).then_inc(sems["q_eps"], 1)
                after(dve, "rss", s)
                nc.vector.tensor_tensor(c_col[:, :], beta[:, :], rss[:, :], ALU.mult).then_inc(sems["c_col"], 1)

            def gram(job, dst, s):
                job_filled(dve, job, s)
                after(dve, "decay_set", s)
                after(dve, "c_col", s)
                nc.vector.scalar_tensor_tensor(dst[:, 0:2 * P], bank(job)[:, 0:2 * P], c_col[:, 0:1], decay[:, 0:2 * P],
                                               ALU.mult, ALU.mult)
                nc.vector.scalar_tensor_tensor(dst[:, 2 * P:3 * P], bank(job)[:, 2 * P:3 * P], c_col[:, 1:2],
                                               decay[:, 2 * P:3 * P], ALU.mult, ALU.mult).then_inc(empty(job), 1)

            def t0(s):
                after(dve, "ct", s, 1)
                nc.vector.tensor_tensor(inv[:, 1, :, :], ident.unsqueeze(1).to_broadcast([P, TT, P]), ct[:, 0, :, :],
                                        ALU.subtract).then_inc(sems["s0"], 1)

            def merge(lv, s):
                job_filled(dve, f"tct{lv}", s)
                for side in range(0 if lv < LEVELS - 1 else 1, 2):
                    view = level_cols(inv[:, side, :, :], lv, side)
                    ins = nc.vector.tensor_tensor(view, view, bank(f"tct{lv}")[:, side * P:(side + 1) * P].rearrange(
                        "p (t b i) -> p t b i", t=TT, i=1 << lv), ALU.subtract)
                ins.then_inc(empty(f"tct{lv}"), 1)

            def r1(s):
                job_filled(dve, "r1", s)
                job_emptied(dve, "vt1", s)
                nc.vector.tensor_tensor(rhs1[:, :], v_tok[:, 1, :], bank("r1")[:, :], ALU.subtract).then_inc(empty("r1"), 1)

            def o(s):
                after(dve, "o_ss", s)
                nc.vector.scalar_tensor_tensor(o_arg[:, :], o_ss[:, :], 1.0 / D, q_eps[:, :], ALU.mult,
                                               ALU.add).then_inc(sems["o_arg"], 1)
                after(dve, "o_scale", s)
                after(dve, "gate_w", s)
                for t in range(TT):
                    job_filled(dve, f"o{t}", s)
                    nc.vector.scalar_tensor_tensor(v_tok[:, t, :], bank(f"o{t}")[:, :], o_scale[:, t:t + 1], gate[:, t, :],
                                                   ALU.mult, ALU.mult).then_inc(empty(f"o{t}"), 1)

            def h_add(s):
                def add(t):
                    job_filled(dve, f"h{t}", s)
                    nc.vector.scalar_tensor_tensor(h[:, t, :], bank(f"h{t}")[:, :], UNDO_AW, h[:, t, :], ALU.mult,
                                                   ALU.add).then_inc(empty(f"h{t}"), 1)
                    job_emptied(dve, f"h{t}", s)

                layer_norm(h, add, 1, ("stats2", "moments2", "mean2", "gap_sq2", "m22", "var_e2", "rstd2", "yn"),
                           lambda: None, s)

            def hidden(f, r):
                after(dve, "silu", r, f + 1)
                if f >= 2:
                    after(dve, "hid_lo", r, f - 1)
                nc.vector.scalar_tensor_tensor(hid[:, f % 2, :], bank(f"gu{f}")[:, T:2 * T], UNDO_AW * H_UP,
                                               silu[:, f % 2, :], ALU.mult, ALU.mult).then_inc(empty(f"gu{f}"), 1)

            def result_add(r):
                after(dve, "kept", r)
                after(dve, "result_free", r, 1)
                for t in range(TT):
                    job_filled(dve, f"down{t}", r)
                    nc.vector.scalar_tensor_tensor(result[:, t, :], bank(f"down{t}")[:, :], UNDO_HW, h2[:, t, :], ALU.mult,
                                                   ALU.add).then_inc(empty(f"down{t}"), 1)

            att = dict(dft0=lambda s: halves_joined(0, s), dft1=dft, xt=lambda s: lows("xt", xt_lo, xt_hi, "xt_hi", 1.0, s), ba=ba,
                       k=lambda s: taps("k", s), q=lambda s: taps("q", s), v=lambda s: taps("v", s), norm=norm,
                       kk=lambda s: gram("kk", nt, s), qk=lambda s: gram("qk", pt, s), t0=t0, r1=r1, o=o,
                       ot=lambda s: lows("ot", xt_lo, xt_hi, "og_hi", A_UP, s), h=h_add)

            def body(s, r):
                for stage in STAGES:
                    if stage in att and s is not None:
                        att[stage](s)
                    elif stage == "yt" and r is not None:
                        lows("yt", yt_lo, yt_hi, "yt_hi", 1.0, r)
                    elif stage[:3] == "tct" and s is not None:
                        merge(int(stage[-1]), s)
                    elif stage[0] == "u" and r is not None:
                        hidden(int(stage[1:]), r)
                    elif stage == "out" and r is not None:
                        result_add(r)

            run(dve, body)


def build(nc, x, sqrt_eig, pct, w_all, dft, consts, conv, ba, norm, gate, out):
    z = nc.dram_tensor("z_rows", [2 * (ORDERS - 1), SEQS, T], F32, kind="Internal").ap()
    with ExitStack() as ctx:
        banks = [ctx.enter_context(nc.psum_tensor(f"bank{i}", [P, 512], F32)) for i in range(8)]
        w_hi = ctx.enter_context(nc.sbuf_tensor("w_hi", [P, ALL_COLS], F16))
        w_lo = ctx.enter_context(nc.sbuf_tensor("w_lo", [P, ALL_COLS], F16))
        load_phase(nc, banks, x, sqrt_eig, pct, z, w_all, w_hi, w_lo)
        sequence_phase(nc, banks, z, dft, consts, dict(conv=conv, ba=ba, norm=norm, gate=gate), w_hi, w_lo, out)


def shape_constants():
    n = 2 * NLAT
    j = np.arange(n)
    m = np.arange(NLAT)
    ang = 2 * np.pi * ((m[:, None] * j[None]) % n) / n
    re = np.where(m[:, None] == 0, 1.0, 2.0) * np.cos(ang)
    im = -2.0 * np.sin(ang)
    im[0] = np.cos(np.pi * j)
    dft = np.concatenate([re[0::2], im[0::2], re[1::2], im[1::2]])[:, :NLAT].astype(np.float32)
    i = np.arange(P)
    mats = [np.eye(P), i[:, None] <= i[None], np.ones((P, P)), i[:, None] > i[None]]
    for lv in range(LEVELS):
        b = i >> lv
        mats.append((b[:, None] % 2 == 0) & (b[None] == b[:, None] + 1))
    return dft, np.concatenate([a.astype(np.float32) for a in mats], 1)


def kernel(**inputs):
    import numpy as _np
    import concourse.bacc as _bacc
    from concourse import mybir as _mybir
    from concourse.bass_utils import run_bass_kernel_spmd as _run

    a = {k: _np.asarray(v) for k, v in inputs.items()}
    chunked = lambda w: w.T.reshape(-1, P, w.shape[0]).transpose(1, 0, 2).reshape(P, -1)
    names = ["L0_ffn_w_gate", "L0_ffn_w_up", "L0_ffn_w_down"] + [f"L0_attn_{t}_proj_w" for t in "qkvgo"]
    w_all = _np.concatenate([chunked(a[n]) for n in names], 1)
    conv = _np.stack([a[f"L0_attn_{t}_conv_w"].reshape(DC, P, TAPS).transpose(1, 0, 2) for t in "qkv"], 1)
    ba = _np.stack([a["L0_attn_b_proj_w"][0], a["L0_attn_a_proj_w"][0]], 1).reshape(DC, P, 2).transpose(1, 0, 2)
    norm = _np.broadcast_to(a["L0_attn_o_norm_w"], (P, D))
    gate = _np.broadcast_to(_np.stack([a["L0_attn_A_log"][0], a["L0_attn_dt_bias"][0]]), (P, 2))
    dft, consts = shape_constants()
    arrays = dict(x=a["x"], sqrt_eig=a["L0_tok_sqrt_eig"], pct=a["L0_tok_pct"], w_all=w_all, dft=dft, consts=consts,
                  conv=conv, ba=ba, norm=norm, gate=gate)
    arrays = {f"in_{k}": _np.ascontiguousarray(v) for k, v in arrays.items()}
    nc = _bacc.Bacc("TRN2", target_bir_lowering=False, num_devices=1)
    args = [nc.dram_tensor(k, v.shape, _mybir.dt.from_np(v.dtype), kind="ExternalInput").ap() for k, v in arrays.items()]
    out = nc.dram_tensor("out_0", (SEQS, T, D), F32, kind="ExternalOutput").ap()
    build(nc, *args, out)
    r = _run(nc, [arrays], core_ids=[0])
    return r.results[0]["out_0"]
```
